# Optimizing a Trainium2 kernel written in Bass

```python
import numpy as np
import jax
import jax.numpy as jnp

def _softmax(x, axis=-1):
    return jax.nn.softmax(x, axis=axis)

def _gelu(x):
    return jax.nn.gelu(x, approximate=True)

def _silu(x):
    return jax.nn.silu(x)

def _sigmoid(x):
    return jax.nn.sigmoid(x)

def _layernorm(x, axis=-1, eps=1e-05):
    m = jnp.mean(x, axis=axis, keepdims=True)
    v = jnp.var(x, axis=axis, keepdims=True)
    return (x - m) / jnp.sqrt(v + eps)

def _scatter_add(tgt, idx, src, axis=0):
    return tgt.at[idx].add(src)

def _segment_sum(src, seg, n):
    return jax.ops.segment_sum(src, seg, n)
kernel_name = 'mk_macaron_d1_jaxref_r4_28c420'

def setup_inputs(seed: int=0):
    np.random.seed(seed)
    _w = jnp.asarray

    def _L0_attn_setup():
        import jax, jax.numpy as jnp
        import numpy as np
        EMB = 256
        HEADS = 16
        HEADSIZE = EMB // HEADS
        EPS = 1e-05

        def _layernorm(x, g, b):
            m = jnp.mean(x, axis=-1, keepdims=True)
            v = jnp.mean((x - m) ** 2, axis=-1, keepdims=True)
            return (x - m) * jax.lax.rsqrt(v + EPS) * g + b
        key = jax.random.key(seed)
        ks = jax.random.split(key, 6)
        B, T = (4, 512)
        s = 1.0 / np.sqrt(EMB)
        return {'x': jax.random.normal(ks[0], (B, T, EMB), dtype=jnp.float32), 'Wk': jax.random.normal(ks[1], (EMB, EMB), dtype=jnp.float32) * s, 'Wq': jax.random.normal(ks[2], (EMB, EMB), dtype=jnp.float32) * s, 'Wv': jax.random.normal(ks[3], (EMB, EMB), dtype=jnp.float32) * s, 'Wo': jax.random.normal(ks[4], (EMB, EMB), dtype=jnp.float32) * s, 'bo': jnp.zeros((EMB,), dtype=jnp.float32), 'kln_g': jnp.ones((HEADSIZE,), dtype=jnp.float32), 'kln_b': jnp.zeros((HEADSIZE,), dtype=jnp.float32), 'qln_g': jnp.ones((HEADSIZE,), dtype=jnp.float32), 'qln_b': jnp.zeros((HEADSIZE,), dtype=jnp.float32)}
    _L0_attn_in = _L0_attn_setup()

    def _L0_ffn_setup():
        import jax, jax.numpy as jnp
        import numpy as np
        B, S, D = (8, 1024, 256)
        E, R, K = (6, 16, 2)
        key = jax.random.key(seed)
        ks = jax.random.split(key, 9)
        sc = 0.02
        return {'x': jax.random.normal(ks[0], (B, S, D), jnp.float32), 'base_W': jax.random.normal(ks[1], (D, D), jnp.float32) * sc, 'base_b': jax.random.normal(ks[2], (D,), jnp.float32) * sc, 'shared_A': jax.random.normal(ks[3], (R, D), jnp.float32) * sc, 'shared_B': jax.random.normal(ks[4], (D, R), jnp.float32) * sc, 'routed_A': jax.random.normal(ks[5], (E, R, D), jnp.float32) * sc, 'routed_B': jax.random.normal(ks[6], (E, D, R), jnp.float32) * sc, 'router_W': jax.random.normal(ks[7], (E, D), jnp.float32) * sc, 'router_b': jax.random.normal(ks[8], (E,), jnp.float32) * sc}
    _L0_ffn_in = _L0_ffn_setup()
    _d = {'L0_attn_x': _L0_attn_in['x'], 'L0_attn_Wk': _L0_attn_in['Wk'], 'L0_attn_Wq': _L0_attn_in['Wq'], 'L0_attn_Wv': _L0_attn_in['Wv'], 'L0_attn_Wo': _L0_attn_in['Wo'], 'L0_attn_bo': _L0_attn_in['bo'], 'L0_attn_kln_g': _L0_attn_in['kln_g'], 'L0_attn_kln_b': _L0_attn_in['kln_b'], 'L0_attn_qln_g': _L0_attn_in['qln_g'], 'L0_attn_qln_b': _L0_attn_in['qln_b'], 'L0_ffn_base_W': _L0_ffn_in['base_W'], 'L0_ffn_base_b': _L0_ffn_in['base_b'], 'L0_ffn_shared_A': _L0_ffn_in['shared_A'], 'L0_ffn_shared_B': _L0_ffn_in['shared_B'], 'L0_ffn_routed_A': _L0_ffn_in['routed_A'], 'L0_ffn_routed_B': _L0_ffn_in['routed_B'], 'L0_ffn_router_W': _L0_ffn_in['router_W'], 'L0_ffn_router_b': _L0_ffn_in['router_b']}
    _x0 = _d['L0_attn_x']
    _d['L0_attn_x'] = jax.random.normal(jax.random.fold_in(jax.random.key(seed), 1), (1, 4096, 256), dtype=_x0.dtype)
    del _x0
    return _d

def reference(L0_attn_x, L0_attn_Wk, L0_attn_Wq, L0_attn_Wv, L0_attn_Wo, L0_attn_bo, L0_attn_kln_g, L0_attn_kln_b, L0_attn_qln_g, L0_attn_qln_b, L0_ffn_base_W, L0_ffn_base_b, L0_ffn_shared_A, L0_ffn_shared_B, L0_ffn_routed_A, L0_ffn_routed_B, L0_ffn_router_W, L0_ffn_router_b):

    def _L0_attn_ref(x, Wk, Wq, Wv, Wo, bo, kln_g, kln_b, qln_g, qln_b):
        import jax, jax.numpy as jnp
        import numpy as np
        EMB = 256
        HEADS = 16
        HEADSIZE = EMB // HEADS
        EPS = 1e-05

        def _layernorm(x, g, b):
            m = jnp.mean(x, axis=-1, keepdims=True)
            v = jnp.mean((x - m) ** 2, axis=-1, keepdims=True)
            return (x - m) * jax.lax.rsqrt(v + EPS) * g + b
        B, T, E = x.shape
        k = jnp.einsum('bte,fe->btf', x, Wk).reshape(B, T, HEADS, HEADSIZE)
        q = jnp.einsum('bte,fe->btf', x, Wq).reshape(B, T, HEADS, HEADSIZE)
        v = jnp.einsum('bte,fe->btf', x, Wv).reshape(B, T, HEADS, HEADSIZE)
        k = _layernorm(k, kln_g, kln_b)
        q = _layernorm(q, qln_g, qln_b)
        scale = E ** (-0.25)
        q = q * scale
        k = k * scale
        dot = jnp.einsum('bihd,bjhd->bhij', q, k)
        causal = jnp.triu(jnp.ones((T, T), dtype=bool), k=1)
        dot = jnp.where(causal, -jnp.inf, dot)
        att = jax.nn.softmax(dot, axis=-1)
        out = jnp.einsum('bhij,bjhd->bihd', att, v).reshape(B, T, E)
        return jnp.einsum('bte,fe->btf', out, Wo) + bo

    def _L0_ffn_ref(x, base_W, base_b, shared_A, shared_B, routed_A, routed_B, router_W, router_b):
        import jax, jax.numpy as jnp
        import numpy as np
        B, S, D = (8, 1024, 256)
        E, R, K = (6, 16, 2)
        base_out = jax.lax.stop_gradient(jnp.einsum('bsi,oi->bso', x, base_W) + base_b)
        shared_out = jnp.einsum('bsr,or->bso', jnp.einsum('bsi,ri->bsr', x, shared_A), shared_B)
        logits = jnp.einsum('bsi,ei->bse', x, router_W) + router_b
        gate = jax.nn.softmax(logits, axis=-1)
        topk_w, topk_i = jax.lax.top_k(gate, K)
        sparse_w = jnp.sum(jax.nn.one_hot(topk_i, E, dtype=gate.dtype) * topk_w[..., None], axis=-2)
        sparse_w = sparse_w / (jnp.sum(sparse_w, axis=-1, keepdims=True) + 1e-06)
        h = jnp.einsum('bsi,eri->bser', x, routed_A)
        routed_outs = jnp.einsum('bser,eor->bseo', h, routed_B)
        routed_out = jnp.einsum('bseo,bse->bso', routed_outs, sparse_w)
        return base_out + shared_out + routed_out
    x = L0_attn_x
    x = x + 0.5 * _L0_ffn_ref(_layernorm(x, axis=-1), L0_ffn_base_W, L0_ffn_base_b, L0_ffn_shared_A, L0_ffn_shared_B, L0_ffn_routed_A, L0_ffn_routed_B, L0_ffn_router_W, L0_ffn_router_b)
    x = x + _L0_attn_ref(_layernorm(x, axis=-1), L0_attn_Wk, L0_attn_Wq, L0_attn_Wv, L0_attn_Wo, L0_attn_bo, L0_attn_kln_g, L0_attn_kln_b, L0_attn_qln_g, L0_attn_qln_b)
    x = x + 0.5 * _L0_ffn_ref(_layernorm(x, axis=-1), L0_ffn_base_W, L0_ffn_base_b, L0_ffn_shared_A, L0_ffn_shared_B, L0_ffn_routed_A, L0_ffn_routed_B, L0_ffn_router_W, L0_ffn_router_b)
    return x

_drawn_inputs = setup_inputs


def setup_inputs(seed=0):
    import zlib

    import numpy as np

    out = dict(_drawn_inputs(seed))
    spreads = {'L0_attn_bo': (0.0, 0.1),
     'L0_attn_kln_g': (1.0, 0.6),
     'L0_attn_kln_b': (0.0, 2.0),
     'L0_attn_qln_g': (1.0, 0.6),
     'L0_attn_qln_b': (0.0, 2.0)}
    factors = {'L0_attn_Wk': 2.803,
     'L0_attn_Wq': 2.767,
     'L0_ffn_routed_A': 3.387,
     'L0_ffn_routed_B': 3.393,
     'L0_ffn_router_W': 4.249,
     'L0_ffn_router_b': 8.0}
    for name, (base, spread) in spreads.items():
        noise = np.random.default_rng([zlib.crc32(name.encode()), seed]).standard_normal(out[name].shape)
        drawn = base * np.exp(spread * noise) if base else spread * noise
        out[name] = jnp.asarray(drawn.astype(out[name].dtype))
    for name, factor in factors.items():
        out[name] = (out[name] * factor).astype(out[name].dtype)
    return out
```

```python
import concourse.bass as bass
from concourse import mybir
from contextlib import ExitStack

F32 = mybir.dt.float32
F32R = mybir.dt.float32r
BF16 = mybir.dt.bfloat16
I32 = mybir.dt.int32
ALU = mybir.AluOpType
ACTF = mybir.ActivationFunctionType
AX = mybir.AxisListType


class Program:

    def __init__(self, nc, ctx):
        self.nc, self.ctx = nc, ctx
        self.queues = {"pe": [], "dve": [], "act": [], "pool": [], "sp": []}
        self.sems, self.counts, self.owner = {}, {}, {}
        self.waited = {e: {} for e in self.queues}

    def bump(self, name, by, eng):
        if name not in self.sems:
            self.sems[name] = self.ctx.enter_context(self.nc.semaphore(name))
            self.counts[name] = 0
            self.owner[name] = eng
        assert self.owner[name] == eng, name
        self.counts[name] += by
        return (name, self.counts[name])

    def wait(self, eng, *marks):
        for mark in marks:
            if mark is None:
                continue
            name, value = mark
            if self.waited[eng].get(name, 0) >= value:
                continue
            self.waited[eng][name] = value
            sem = self.sems[name]
            self.queues[eng].append(lambda e, sem=sem, value=value: e.wait_ge(sem, value))

    def do(self, eng, issue, after=(), says=None, by=1):
        self.wait(eng, *after)
        if says is None:
            self.queues[eng].append(issue)
            return None
        mark = self.bump(says, by, eng)
        sem = self.sems[says]
        self.queues[eng].append(lambda e: issue(e).then_inc(sem, by))
        return mark

    def dma(self, eng, out, in_, says, after=()):
        return self.do(eng, lambda e: e.dma_start(out, in_), after, says, 16)

    def only_if_zero(self, eng, flag):
        self.queues[eng].append(("if_zero", flag))
        self.saved = dict(self.saved) if hasattr(self, "saved") else {}
        self.saved[eng] = dict(self.waited[eng])

    def end_if(self, eng):
        self.queues[eng].append(("end", None))
        self.waited[eng] = self.saved[eng]

    def emit(self, eng, e):
        guard = None
        for item in self.queues[eng]:
            if isinstance(item, tuple):
                if item[0] == "if_zero":
                    flag = e.value_load(item[1], min_val=0, max_val=1)
                    guard = e.If(flag == 0)
                    guard.__enter__()
                else:
                    guard.__exit__(None, None, None)
            else:
                item(e)


def build(nc, ap, out, always_general=False):
    T, D = 4096, 256
    P = 128
    NT = T // P
    NH, HS = 16, 16
    NE, R = 6, 16
    NR = (NE + 1) * R
    NA = NR + NE
    EPS = 1e-5
    GT = 8
    CH = 512
    NC = T // CH
    TC = CH // P
    PARTS = 3
    Q_PARTS = [0, 0, 1, 1, 0, 2]
    K_PARTS = [0, 1, 0, 1, 2, 0]
    KR = len(Q_PARTS) * HS
    KS = KR + PARTS
    VO = HS
    VW = 3 * HS + 1
    VL = HS + 1
    UB = 3
    UW = UB * CH
    NEG = -1e30
    SAFE = 60.0
    SCALE = float(D) ** -0.25

    ctx = ExitStack()
    with ctx:
        pr = Program(nc, ctx)

        def sb(name, shape, dt=F32):
            return ctx.enter_context(nc.sbuf_tensor(name, shape, dt))

        def dram(name, shape, dt):
            return nc.dram_tensor(name, shape, dt, kind="Internal").ap()

        parts_d = dram("parts_d", [PARTS, 4, P, T], BF16)
        shift_d = dram("shift_d", [NH, PARTS, T], BF16)

        x = sb("x", [P, NT, D])
        wide = sb("wide", [P, 2, T])
        xnT = wide
        wide_b = wide[:, :, :].rearrange("p a t -> p (a t)").bitcast(BF16)
        ops = wide_b.rearrange("p (s a t) -> p s a t", s=2, a=2)
        ring = sb("ring", [P, 3 * UW])
        probs = ring[:, 0:3 * UW].rearrange("p (s c) -> p s c", s=3)
        rest = sb("rest", [P, 3, UW], F32R)
        HB = 120
        h_all = ring[:, 0:NT * HB].rearrange("p (n c) -> p n c", n=NT)
        big = sb("big", [P, NT * NH * VL])
        o_all = big[:, :].rearrange("p (n h c) -> p n h c", n=NT, h=NH)
        stage = big[:, 0:2 * PARTS * 4 * CH // 2].bitcast(BF16).rearrange(
            "p (s r b t) -> p s r b t", s=2, r=PARTS, b=4)
        vhi_f = sb("vhi", [P, NT * NH * VW], BF16)
        vhi = vhi_f[:, :].rearrange("p (n h c) -> p n h c", n=NT, h=NH)
        vlo = sb("vlo", [P, 2, NT, VL], F32R)

        ident = sb("ident", [P, P])
        identb = sb("identb", [P, P], BF16)
        maskT = sb("maskT", [P, P], BF16)
        maskN = sb("maskN", [P, P], BF16)
        tri = sb("tri", [P, NE, NE])
        pick = sb("pick", [VW, VL])
        eps = sb("eps", [P, 1])
        wraw = vhi_f[:, 0:3 * 2 * D * 2].bitcast(F32).rearrange("p (s a d) -> p s a d", s=3, a=2)
        baseT = sb("baseT", [P, 2, D])
        aT = sb("aT", [P, 2, NA])
        bT = sb("bT", [NR + 1, D])
        WB = 2 * PARTS * 4 * CH // 2
        qkT = big[:, WB:WB + 4 * D].rearrange("p (a d) -> p a d", a=2)
        vT = big[:, WB + 4 * D:WB + 6 * D].rearrange("p (a d) -> p a d", a=2)
        woT = sb("woT", [P, 2, D])
        wmean = sb("wmean", [P, 2, 2 * NH])
        rb = sb("rb", [P, NE])
        bo = sb("bo", [P, D])
        gb = sb("gb", [P, 4])
        gbr = sb("gbr", [1, 4, HS])
        bound = sb("bound", [1, 16])
        flag = sb("flag", [1, 1], I32)
        st = sb("st", [P, NT, 6])
        mv = sb("mv", [P, NT, 2])
        rstd = sb("rstd", [P, NT])
        mix = sb("mix", [P, 2 * D + 2 * GT * NE * NE])
        xn = mix[:, 0:2 * D].rearrange("p (s d) -> p s d", s=2)
        gt, eq = (mix[:, 2 * D + i * GT * NE * NE:2 * D + (i + 1) * GT * NE * NE].rearrange(
            "p (n e f) -> p n e f", n=GT, e=NE) for i in range(2))
        oT = mix[0:VW, 0:2 * CH].rearrange("p (s c) -> p s c", s=2)
        lg = sb("lg", [P, GT, NE])
        ex = sb("ex", [P, GT, NE])
        r3 = sb("r3", [P, 4, GT])
        rank = sb("rank", [P, GT, NE])
        wt = sb("wt", [P, NT, NE + 1])
        hw = sb("hw", [P, 2, NR + 1])
        hT = sb("hT", [NR + 1, 2, P])
        sq = ring[:, 0:2 * CH].rearrange("p (s c) -> p s c", s=2)
        qn = ring[:, 2 * CH:4 * CH].rearrange("p (s c) -> p s c", s=2)
        qT = ring[:, 4 * CH:6 * CH].rearrange("p (s c) -> p s c", s=2)
        qr = ring[:, 6 * CH:8 * CH].rearrange("p (s c) -> p s c", s=2)
        vr = ring[:, 8 * CH:9 * CH].rearrange("p (s c) -> p s c", s=2)
        ss = sb("ss", [P, 2, 2 * NH])
        den = sb("den", [P, GT, NH])
        at = vhi_f[:, 0:2 * D * 2].bitcast(F32).rearrange("p (s d) -> p s d", s=2)
        atT = vhi_f[:, 2 * D * 2:4 * D * 2].bitcast(F32).rearrange("p (s a t) -> p s a t", s=2, a=2)
        mx2 = sb("mx2", [P, NT, 2])
        mx = sb("mx", [P, NT])
        mres = sb("mres", [P, 2, NT])
        mparts = sb("mparts", [P, PARTS, NT], BF16)
        mT = sb("mT", [PARTS * NT, P], BF16)

        ps = ctx.enter_context(nc.psum_tensor("ps", [P, 8 * CH], F32))

        def bank(b, n=1):
            return ps[:, b * CH:(b + n) * CH]

        bank_free = [None] * 8

        def mm(o, lhsT, rhs, start, stop, after=(), says=None):
            return pr.do("pe", lambda e: e.matmul(o, lhsT, rhs, start=start, stop=stop, skip_group_check=True), after, says)

        def tr(o, in_, idn, after=(), says=None):
            return pr.do("pe", lambda e: e.transpose(o, in_, idn), after, says)

        def act(o, in_, f, after=(), says=None, bias=0.0, scale=1.0):
            if f == ACTF.Copy:
                return pr.do("act", lambda e: e.activation(o, in_, f), after, says)
            return pr.do("act", lambda e: e.activation(o, in_, f, bias=bias, scale=scale), after, says)

        def tt(eng, o, a, b, op, after=(), says=None):
            return pr.do(eng, lambda e: e.tensor_tensor(o, a, b, op), after, says)

        def tsc(eng, o, a, s1, s2, op0, op1, after=(), says=None):
            if s2 is None:
                return pr.do(eng, lambda e: e.tensor_scalar(o, a, s1, None, op0), after, says)
            return pr.do(eng, lambda e: e.tensor_scalar(o, a, s1, s2, op0, op1), after, says)

        def stt(o, a, s, b, op0, op1, after=(), says=None):
            return pr.do("dve", lambda e: e.scalar_tensor_tensor(out=o, in0=a, scalar=s, in1=b, op0=op0, op1=op1), after, says)

        def red(o, a, op, after=(), says=None, absolute=False):
            if absolute:
                return pr.do("dve", lambda e: e.tensor_reduce(o, a, AX.X, op, apply_absolute_value=True), after, says)
            return pr.do("dve", lambda e: e.tensor_reduce(o, a, AX.X, op), after, says)

        def recip(o, a, after=(), says=None):
            return pr.do("dve", lambda e: e.reciprocal(o, a), after, says)

        def copy(eng, o, a, after=(), says=None):
            return pr.do(eng, lambda e: e.tensor_copy(o, a), after, says)

        def memset(eng, o, v, after=(), says=None):
            return pr.do(eng, lambda e: e.memset(o, v), after, says)

        def select(o, pattern, cm, base, op, fill, after=(), says=None):
            return pr.do("pool", lambda e: e.affine_select(out=o, in_=o, compare_op=op, fill=fill, base=base,
                                                           pattern=pattern, channel_multiplier=cm), after, says)

        z = memset("pool", ident[:, :], 0.0, says="const")
        ident_ok = select(ident[:, :], [[-1, P]], 1, 0, ALU.not_equal, 1.0, [z], "const")
        z = memset("pool", identb[:, :], 0.0, says="const")
        select(identb[:, :], [[-1, P]], 1, 0, ALU.not_equal, 1.0, [z], "const")
        z = memset("pool", maskT[:, :], 0.0, says="const")
        select(maskT[:, :], [[1, P]], -1, 0, ALU.is_ge, NEG, [z], "const")
        z = memset("pool", maskN[:, :], 0.0, says="const")
        select(maskN[:, :], [[-1, P]], 1, 0, ALU.is_ge, NEG, [z], "const")
        z = memset("pool", tri[:, :, :], 0.0, says="const")
        select(tri[:, :, :], [[-1, NE], [1, NE]], 0, 0, ALU.is_ge, 1.0, [z], "const")
        z = memset("pool", pick[:, :], 0.0, says="const")
        z = select(pick[:, :], [[-1, VL]], 1, 0, ALU.not_equal, 1.0, [z], "const")
        z = select(pick[:, 0:HS], [[-1, HS]], 1, -(HS + 1), ALU.not_equal, 1.0, [z], "const")
        z = select(pick[:, 0:HS], [[-1, HS]], 1, -(2 * HS + 1), ALU.not_equal, 1.0, [z], "const")
        memset("pool", eps[:, :], EPS, says="const")
        memset("pool", wt[:, :, 0:1], 1.0, says="const")
        memset("pool", hw[:, :, NR:NR + 1], 1.0, says="const")
        memset("pool", mT[:, :], 0.0, says="const")
        const_ok = memset("pool", vlo[:, :, :, VO:VO + 1].bitcast(F32), 1.0, says="const")

        x_v = ap["x"][0].rearrange("(n p) d -> p n d", p=P)
        LT = 4
        x_in = []
        for i in range(NT // LT):
            x_in.append(pr.dma("sp", x[:, i * LT:(i + 1) * LT, :], x_v[:, i * LT:(i + 1) * LT, :], f"x_in{i}"))
        half = lambda w: w.rearrange("(b p) e -> p b e", p=P)
        A_RAW, B_RAW = 1, 2
        pr.dma("act", wraw[:, 0, :, :], half(ap["base_W"]), "w_base")
        w_base = ("w_base", 16)
        raw_a = wraw[:, A_RAW, 0, :]
        raw_b = wraw[:, B_RAW, :, 0:NR]
        pr.dma("act", raw_a[0:R, :], ap["shared_A"], "w_a")
        pr.dma("act", raw_a[R:NR, :], ap["routed_A"].rearrange("e r d -> (e r) d"), "w_a")
        w_a = pr.dma("act", raw_a[NR:NA, :], ap["router_W"], "w_a")
        pr.dma("act", raw_b[:, :, 0:R], ap["shared_B"].rearrange("(b p) r -> p b r", p=P), "w_b")
        for e_ in range(NE):
            w_b = pr.dma("act", raw_b[:, :, R + e_ * R:R + (e_ + 1) * R],
                         ap["routed_B"][e_].rearrange("(b p) r -> p b r", p=P), "w_b")
        w_bias = pr.dma("act", bT[NR:NR + 1, :], ap["base_b"].rearrange("(a n) -> a n", a=1), "w_bias")
        pr.dma("act", rb[:, :], ap["router_b"].partition_broadcast(P), "w_vec")
        w_vec = pr.dma("act", bo[:, :], ap["bo"].partition_broadcast(P), "w_vec")
        for i, name in enumerate(["qln_g", "qln_b", "kln_g", "kln_b"]):
            for h in range(P // HS):
                pr.dma("sp", gb[h * HS:(h + 1) * HS, i:i + 1], ap[name].rearrange("(a n) -> a n", n=1), "gb_in")
            gb_in = pr.dma("sp", gbr[:, i, :], ap[name].rearrange("(a n) -> a n", a=1), "gb_in")
        shift_zero = None
        for h in range(NH):
            shift_zero = pr.dma("sp", shift_d[h].rearrange("r (n t) -> (r n) t", t=P), mT[:, :], "shift_in", [const_ok])

        sc = pr.do("dve", lambda e: e.tensor_scalar_mul(gb[:, :], gb[:, :], SCALE), [gb_in], "bnd")
        red(bound[:, 0:4].unsqueeze(2), gbr[:, :, :], ALU.max, [gb_in], "bnd", absolute=True)
        b1 = red(bound[:, 0:4].unsqueeze(2), gbr[:, :, :], ALU.max, [("bnd", pr.counts["bnd"])], "bnd", absolute=True)
        b2 = tt("dve", gbr[:, :, :], gbr[:, :, :], gbr[:, :, :], ALU.mult, [b1], "bnd")
        b3 = red(bound[:, 4:8].unsqueeze(2), gbr[:, :, :], ALU.add, [b2], "bnd")
        b4 = act(bound[:, 8:12], bound[:, 4:8], ACTF.Sqrt, [b3], "bnd_sqrt")
        bv = bound[:, :].rearrange("a (k b c) -> a k b c", k=4, c=2)
        b5 = stt(bound[:, 12:14], bv[:, 0, :, 0], float(HS) ** 0.5, bv[:, 2, :, 1], ALU.mult, ALU.add, [b4], "bnd")
        b6 = tt("dve", bound[:, 14:15], bound[:, 12:13], bound[:, 13:14], ALU.mult, [b5], "bnd")
        limit = -1.0 if always_general else SAFE
        b7 = tsc("dve", bound[:, 15:16], bound[:, 14:15], SCALE * SCALE, limit, ALU.mult, ALU.is_le, [b6], "bnd")
        flag_ok = copy("dve", flag[:, :], bound[:, 15:16], [b7], "bnd")

        bank_turn = [0]

        def transpose_in(dst, src, rows, after, n_cols=P):
            b = bank_turn[0] % 4
            bank_turn[0] += 1
            t = tr(bank(b)[0:n_cols, 0:rows], src, ident[0:rows, 0:rows], list(after) + [bank_free[b]], "w_tr")
            bank_free[b] = copy("dve", dst, bank(b)[0:n_cols, 0:rows], [t], "w_cp")
            return bank_free[b]

        for ob in range(2):
            for ib in range(2):
                transpose_in(baseT[:, ib, ob * P:(ob + 1) * P], wraw[:, 0, ob, ib * P:(ib + 1) * P], P, [w_base, const_ok])
        for ib in range(2):
            transpose_in(aT[:, ib, :], raw_a[0:NA, ib * P:(ib + 1) * P], NA, [w_a])
        for ob in range(2):
            ffn_w = transpose_in(bT[0:NR, ob * P:(ob + 1) * P], raw_b[:, ob, :], P, [w_b], NR)
        pe_done = ("w_tr", pr.counts["w_tr"])

        def load_weight(slot, name, free, reload):
            return pr.dma("act", wraw[:, slot, :, :], half(ap[name]), f"w_in_{name}", [free])

        wq_in = load_weight(0, "Wq", pe_done, True)
        wk_in = load_weight(1, "Wk", pe_done, True)
        wv_in = load_weight(2, "Wv", pe_done, True)

        def attention_weights():
            for slot, dst, off, ready in ((0, qkT, 0, wq_in), (1, qkT, D, wk_in), (2, vT, 0, wv_in)):
                for ob in range(2):
                    for ib in range(2):
                        m = transpose_in(dst[:, ib, off + ob * P:off + (ob + 1) * P],
                                         wraw[:, slot, ob, ib * P:(ib + 1) * P], P, [ready])
            used = ("w_tr", pr.counts["w_tr"])
            wo_in = load_weight(0, "Wo", used, True)
            for ob in range(2):
                for ib in range(2):
                    m = transpose_in(woT[:, ib, ob * P:(ob + 1) * P], wraw[:, 0, ob, ib * P:(ib + 1) * P], P, [wo_in])
            a1 = red(wmean[:, :, :].rearrange("p a (h c) -> p (a h) c", c=1), qkT[:, :, :].rearrange("p a (h c) -> p (a h) c", c=HS), ALU.add, [m], "w_mean")
            a2 = pr.do("dve", lambda e: e.tensor_scalar_mul(wmean[:, :, :], wmean[:, :, :], 1.0 / HS), [a1], "w_mean")
            for ib in range(2):
                a3 = tt("dve", qkT[:, ib, :].rearrange("p (h c) -> p h c", c=HS), qkT[:, ib, :].rearrange("p (h c) -> p h c", c=HS),
                        wmean[:, ib, :].unsqueeze(2).broadcast_to([P, 2 * NH, HS]), ALU.subtract, [a2], "w_mean")
            return a3

        def stats(n0, n1, ready):
            for n in range(n0, n1):
                s = pr.do("dve", lambda e, n=n: e.bn_stats(st[:, n, :], x[:, n, :]), [ready(n)], "ln_st")
            for n in range(n0, n1):
                s2 = pr.do("dve", lambda e, n=n: e.bn_aggr(mv[:, n, :], st[:, n, :]), [s], "ln_st")
            s3 = act(rstd[:, n0:n1], mv[:, n0:n1, 1], ACTF.Sqrt, [s2], "ln_sqrt", bias=eps[:, :])
            return recip(rstd[:, n0:n1], rstd[:, n0:n1], [s3], "ln_r")

        xn_free = [None, None]
        xt_free = [None, None]

        def normalise(n, ready, free=()):
            s = n % 2
            a = tsc("dve", xn[:, s, :], x[:, n, :], mv[:, n, 0:1], rstd[:, n:n + 1], ALU.subtract, ALU.mult,
                    [ready, xn_free[s]], "xn")
            for ib in range(2):
                t = tr(bank(s)[:, ib * P:(ib + 1) * P], xn[:, s, ib * P:(ib + 1) * P], ident[:, :], [a, bank_free[s]], "xn_tr")
            xn_free[s] = t
            c = act(xnT[:, :, n * P:(n + 1) * P], bank(s)[:, 0:2 * P].rearrange("p (a t) -> p a t", a=2), ACTF.Copy,
                    [t] + list(free), "xnT")
            bank_free[s] = c
            return c

        out_v = out[0].rearrange("(n p) d -> p n d", p=P)

        def feed_forward(ready, after_weights, final):
            h_free, w_free = None, None
            done = []
            hw_free = [None, None]
            hT_free = [None, None]
            for g in range(NT // GT):
                n0 = g * GT
                r = stats(n0, n0 + GT, ready)
                for n in range(n0, n0 + GT):
                    c = normalise(n, r)
                    b = 2 + n % 2
                    for ib in range(2):
                        m = mm(bank(b)[:, 0:NA], xnT[:, ib, n * P:(n + 1) * P], aT[:, ib, :], ib == 0, ib == 1,
                               [c, after_weights, bank_free[b]], "ff_a")
                    hc = bank_free[b] = act(h_all[:, n, 0:NA], bank(b)[:, 0:NA], ACTF.Copy, [m], "ff_h")
                tiles = slice(n0, n0 + GT)
                a = tt("dve", lg[:, :, :], h_all[:, tiles, NR:NA], rb[:, :].unsqueeze(1).broadcast_to([P, GT, NE]), ALU.add, [hc, w_vec], "rt")
                a = red(r3[:, 0, :].unsqueeze(2), lg[:, :, :], ALU.max, [a], "rt")
                a = tt("dve", lg[:, :, :], lg[:, :, :], r3[:, 0, :].unsqueeze(2).broadcast_to([P, GT, NE]), ALU.subtract, [a], "rt")
                a = act(ex[:, :, :], lg[:, :, :], ACTF.Exp, [a], "rt_exp")
                red(r3[:, 1, :].unsqueeze(2), ex[:, :, :], ALU.add, [a], "rt")
                other = ex[:, :, :].unsqueeze(2).broadcast_to([P, GT, NE, NE])
                own = ex[:, :, :].unsqueeze(3).broadcast_to([P, GT, NE, NE])
                tt("dve", gt[:, :, :, :], other, own, ALU.is_gt, [a], "rt")
                a = tt("dve", eq[:, :, :, :], other, own, ALU.is_equal, [a], "rt")
                a = tt("dve", eq[:, :, :, :], eq[:, :, :, :], tri[:, :, :].unsqueeze(1).broadcast_to([P, GT, NE, NE]), ALU.mult, [a, const_ok], "rt")
                a = tt("dve", gt[:, :, :, :], gt[:, :, :, :], eq[:, :, :, :], ALU.add, [a], "rt")
                a = red(rank[:, :, :].unsqueeze(3), gt[:, :, :, :], ALU.add, [a], "rt")
                a = stt(rank[:, :, :], rank[:, :, :], 2.0, ex[:, :, :], ALU.is_lt, ALU.mult, [a], "rt")
                a = red(r3[:, 2, :].unsqueeze(2), rank[:, :, :], ALU.add, [a], "rt")
                a = stt(r3[:, 3, :], r3[:, 1, :], 1e-6, r3[:, 2, :], ALU.mult, ALU.add, [a], "rt")
                a = recip(r3[:, 3, :], r3[:, 3, :], [a], "rt")
                wts = tt("dve", wt[:, tiles, 1:NE + 1], rank[:, :, :], r3[:, 3, :].unsqueeze(2).broadcast_to([P, GT, NE]), ALU.mult, [a], "rt")
                for n in range(n0, n0 + GT):
                    s = n % 2
                    a = tt("dve", hw[:, s, 0:NR].rearrange("p (e r) -> p e r", r=R), h_all[:, n, 0:NR].rearrange("p (e r) -> p e r", r=R),
                           wt[:, n, :].unsqueeze(2).broadcast_to([P, NE + 1, R]), ALU.mult, [wts, hw_free[s]], "ff_w")
                    b = 4 + s
                    hw_free[s] = t = tr(bank(b)[0:NR + 1, 0:P], hw[:, s, :], ident[:, :], [a, bank_free[b]], "ff_tr")
                    c = bank_free[b] = act(hT[:, s, :], bank(b)[0:NR + 1, 0:P], ACTF.Copy, [t, hT_free[s]], "ff_hT")
                    b = 6 + s
                    mm(bank(b)[:, 0:D], xnT[:, 0, n * P:(n + 1) * P], baseT[:, 0, :], True, False, [bank_free[b]])
                    mm(bank(b)[:, 0:D], xnT[:, 1, n * P:(n + 1) * P], baseT[:, 1, :], False, False)
                    m = hT_free[s] = mm(bank(b)[:, 0:D], hT[:, s, :], bT[:, :], False, True, [c, w_bias], "ff_o")
                    a = bank_free[b] = stt(x[:, n, :], bank(b)[:, 0:D], 0.5, x[:, n, :], ALU.mult, ALU.add, [m], "ff_x")
                    done.append(a)
                    if final and n % LT == LT - 1:
                        pr.dma("sp", out_v[:, n - LT + 1:n + 1, :], x[:, n - LT + 1:n + 1, :], "out", [a])
            return done

        x1 = feed_forward(lambda n: x_in[n // LT], ffn_w, False)
        w_centred = attention_weights()
        v_ones = memset("pool", vhi[:, :, :, VO:VO + 1], 1.0, [("w_tr", pr.counts["w_tr"])], "v_ones")

        stage_free = [None, None]
        sq_f, qn_f, qT_f, qr_f, vr_f, ss_f = ([None, None] for _ in range(6))
        for g in range(NT // GT):
            n0 = g * GT
            r = stats(n0, n0 + GT, lambda n: x1[n])
            for n in range(n0, n0 + GT):
                s = n % 2
                c = normalise(n, r)
                b = 2 + s
                for ib in range(2):
                    m = mm(bank(b), xnT[:, ib, n * P:(n + 1) * P], qkT[:, ib, :], ib == 0, ib == 1, [c, w_centred, bank_free[b]], "qk")
                for ib in range(2):
                    mv_ = mm(bank(4 + s)[:, 0:D], xnT[:, ib, n * P:(n + 1) * P], vT[:, ib, :], ib == 0, ib == 1, [bank_free[4 + s]], "v")
                a = act(sq[:, s, :], bank(b), ACTF.Square, [m, sq_f[s]], "qk_sq")
                a = sq_f[s] = red(ss[:, s, :].unsqueeze(2), sq[:, s, :].rearrange("p (h c) -> p h c", c=HS), ALU.add, [a, ss_f[s]], "qk_ss")
                a = act(ss[:, s, :], ss[:, s, :], ACTF.Sqrt, [a], "qk_rt", bias=eps[:, :], scale=1.0 / HS)
                a = recip(ss[:, s, :], ss[:, s, :], [a], "qk_ss")
                a = tt("dve", qn[:, s, :].rearrange("p (h c) -> p h c", c=HS), bank(b).rearrange("p (h c) -> p h c", c=HS),
                       ss[:, s, :].unsqueeze(2).broadcast_to([P, 2 * NH, HS]), ALU.mult, [a, qn_f[s]], "qk_n")
                bank_free[b] = ss_f[s] = a
                b = 6 + s
                for k in range(4):
                    t = tr(bank(b)[:, k * P:(k + 1) * P], qn[:, s, k * P:(k + 1) * P], ident[:, :], [a, bank_free[b]], "qk_tr")
                qn_f[s] = t
                tsc("dve", qT[:, s, 0:2 * P], bank(b)[:, 0:2 * P], gb[:, 0:1], gb[:, 1:2], ALU.mult, ALU.add, [t, qT_f[s], sc], "qk_T")
                a = tsc("dve", qT[:, s, 2 * P:], bank(b)[:, 2 * P:], gb[:, 2:3], gb[:, 3:4], ALU.mult, ALU.add, [t], "qk_T")
                bank_free[b] = a
                sg, tc = (n // TC) % 2, n % TC
                part = [stage[:, sg, i, :, tc * P:(tc + 1) * P] for i in range(PARTS)]
                full = qT[:, s, :].rearrange("p (b t) -> p b t", b=4)
                left = qr[:, s, :].rearrange("p (b t) -> p b t", b=4)
                a = act(part[0], full, ACTF.Copy, [a, stage_free[sg]], "cut_a")
                a = qT_f[s] = tt("pool", left, full, part[0], ALU.subtract, [a, qr_f[s]], "cut_p")
                a = act(part[1], left, ACTF.Copy, [a], "cut_a")
                a = qr_f[s] = tt("pool", part[2], left, part[1], ALU.subtract, [a, stage_free[sg]], "cut_p")
                if tc == TC - 1:
                    c0 = (n // TC) * CH
                    for i in range(PARTS):
                        parts_ok = pr.dma("sp", parts_d[i, :, :, c0:c0 + CH].rearrange("b p t -> p b t"), stage[:, sg, i, :, :],
                                          f"parts{sg}", [a])
                    stage_free[sg] = parts_ok
                heads = lambda t_: t_.rearrange("p (h c) -> p h c", c=HS)
                v0, vleft = heads(bank(4 + s)[:, 0:D]), heads(vr[:, s, :])
                a = act(vhi[:, n, :, 0:HS], v0, ACTF.Copy, [mv_], "vcut_a")
                a = bank_free[4 + s] = tt("dve", vleft, v0, vhi[:, n, :, 0:HS], ALU.subtract, [a, vr_f[s]], "vcut_d")
                a = act(vhi[:, n, :, VO + 1:VO + 1 + HS], vleft, ACTF.Copy, [a], "vcut_a")
                a = vr_f[s] = tt("pool", vhi[:, n, :, VO + 1 + HS:VW], vleft, vhi[:, n, :, VO + 1:VO + 1 + HS], ALU.subtract, [a], "vcut_p")
        v_done = a
        x2_ready = [pr.do("pool", lambda e, n=n: e.tensor_tensor(x[:, n, :], x[:, n, :], bo[:, :], ALU.add), [x1[n], r, w_vec, xn_free[0], xn_free[1]], "x_bo") for n in range(NT)]
        prep_pe = [("qk", pr.counts["qk"]), ("v", pr.counts["v"])]
        parts_all = [stage_free[0], stage_free[1]]

        def load_operands(h, slot, rows, sem, after):
            blk, row = h // 8, (h % 8) * HS
            for i, (a_, b_) in enumerate(zip(Q_PARTS, K_PARTS)):
                pr.dma("sp", ops[i * HS:(i + 1) * HS, slot, 0, :], parts_d[a_, blk, row:row + HS, :], sem, after)
                mk = pr.dma("sp", ops[i * HS:(i + 1) * HS, slot, 1, :], parts_d[b_, 2 + blk, row:row + HS, :], sem, after)
            if rows == KS:
                mk = pr.dma("sp", ops[KR:KS, slot, 0, :], shift_d[h], sem, after)
            return mk

        engines = ["pe", "dve", "sp"]
        for e_ in engines:
            pr.wait(e_, flag_ok)
            pr.only_if_zero(e_, flag[0:1, 0:1])
        slot_free = [None, None]
        reg_free = [[bank_free[i] for i in range(4)], [bank_free[i] for i in range(4, 8)]]
        turn = 0
        mT_free = shift_zero
        mp_free = None
        for h in range(NH):
            s = h % 2
            ready = load_operands(h, s, KR, f"gen_in{s}", parts_all + prep_pe + [slot_free[s]])
            last = None
            for n in range(NT):
                width = (n + 1) * P
                for k, j0 in enumerate(range(0, width, 4 * CH)):
                    w = min(4 * CH, width - j0)
                    region = bank(4 * (turn % 2), 4)
                    for c0 in range(0, w, CH):
                        cw = min(CH, w - c0)
                        diag = j0 + c0 + cw == width
                        m = mm(region[:, c0:c0 + cw], ops[0:KR, s, 0, n * P:(n + 1) * P], ops[0:KR, s, 1, j0 + c0:j0 + c0 + cw],
                               True, not diag, [ready] + reg_free[turn % 2], None if diag else "gen_mm")
                        if diag:
                            m = mm(region[:, c0 + cw - P:c0 + cw], identb[:, :], maskN[:, :], False, True, [], "gen_mm")
                    last = red(mx2[:, n, k:k + 1], region[:, 0:w], ALU.max, [m, mp_free], "gen_max")
                    reg_free[turn % 2] = [last]
                    turn += 1
            slot_free[s] = m
            two = NT // 2
            copy("dve", mx[:, 0:two], mx2[:, 0:two, 0], [last], "gen_v")
            a = tt("dve", mx[:, two:], mx2[:, two:, 0], mx2[:, two:, 1], ALU.max, [last], "gen_v")
            a = tsc("dve", mres[:, 0, :], mx[:, :], -1.0, None, ALU.mult, None, [a], "gen_v")
            a = copy("dve", mparts[:, 0, :], mres[:, 0, :], [a], "gen_v")
            a = tt("dve", mres[:, 1, :], mres[:, 0, :], mparts[:, 0, :], ALU.subtract, [a], "gen_v")
            a = copy("dve", mparts[:, 1, :], mres[:, 1, :], [a], "gen_v")
            a = tt("dve", mparts[:, 2, :], mres[:, 1, :], mparts[:, 1, :], ALU.subtract, [a], "gen_v")
            mp_free = a
            b = 4 * (turn % 2)
            t = tr(bank(b)[0:PARTS * NT, 0:P // 2].bitcast(BF16), mparts[:, :, :].rearrange("p r n -> p (r n)"), identb[:, :],
                   [a] + reg_free[turn % 2], "gen_tr")
            a = copy("dve", mT[:, :], bank(b)[0:PARTS * NT, 0:P // 2].bitcast(BF16), [t, mT_free], "gen_v")
            reg_free[turn % 2] = [a]
            turn += 1
            mT_free = pr.dma("sp", shift_d[h].rearrange("r (n t) -> (r n) t", t=P), mT[:, :], "gen_out", [a])
        pr.wait("sp", mT_free)
        pr.wait("pe", *reg_free[0], *reg_free[1])
        gen_last_mm = None
        for e_ in engines:
            pr.end_if(e_)

        units, banks = [], []
        chunk_last = {}
        for h in range(NH):
            for c in range(NC):
                base = TC * c
                rows = [[(j, 0, CH, 0)] for j in range(base + 1)]
                rows.append([(base + 1, P, CH - P, 0), (base + 3, 3 * P, P, CH - P)])
                rows.append([(base + 2, 2 * P, 2 * P, 0)])
                for r_ in rows:
                    banks.append([(h, c) + q for q in r_])
        for i in range(0, len(banks), UB):
            units.append([(q[:5] + (k * CH + q[5],)) for k, bk in enumerate(banks[i:i + UB]) for q in bk])
        seq_last = {}
        for u, un in enumerate(units):
            for i, q in enumerate(un):
                seq_last[(q[0], q[1])] = (u, i)

        ones_rows = memset("dve", ops[KR:KS, :, 1, :], 1.0, [("xnT", pr.counts["xnT"])] + prep_pe, "ones")
        op_ready = {}
        op_free = [prep_pe, prep_pe]

        def fetch(h):
            op_ready[h] = load_operands(h, h % 2, KS, f"op_in{h % 2}", parts_all + [shift_zero] + list(op_free[h % 2]))

        vlo_ready = {}
        vlo_free = [None, None]

        def low_v(h):
            s = h % 2
            vlo_ready[h] = tt("pool", vlo[:, s, :, 0:HS], vhi[:, :, h, 0:HS], vhi[:, :, h, VO + 1:VO + 1 + HS], ALU.add,
                              [v_done, vlo_free[s], const_ok], "vlo")

        for h in range(2):
            fetch(h)
            low_v(h)
        unit_free = [[bank_free[i] for i in range(3)], [bank_free[i] for i in range(3, 6)]]
        acc_free = [bank_free[6], bank_free[7]]
        s_done, e_done, r_done, pv_done = {}, {}, {}, {}
        fetched = 2
        probs_h = ring[:, 0:3 * UW].bitcast(BF16).rearrange("p (s c two) -> p s c two", s=3, two=2)

        def scores(u):
            for i, (h, c, j, c0, w, col) in enumerate(units[u]):
                o = bank(3 * (u % 2), UB)[:, col:col + w]
                diag = j >= TC * c
                last_in = i == len(units[u]) - 1
                q0 = c * CH + c0
                m = mm(o, ops[0:KS, h % 2, 1, j * P:(j + 1) * P], ops[0:KS, h % 2, 0, q0:q0 + w],
                       col % CH == 0, not diag, [op_ready[h], ones_rows] + unit_free[u % 2], None if diag or not last_in else "s")
                if diag:
                    m = mm(o[:, 0:P], identb[:, :], maskT[:, :], False, True, [], "s" if last_in else None)
            s_done[u] = m

        def segments(u):
            segs = []
            for (_, _, _, _, w, col) in units[u]:
                if segs and segs[-1][1] == col:
                    segs[-1][1] = col + w
                else:
                    segs.append([col, col + w])
            return segs

        def exps(u):
            for a, b in segments(u):
                e_done[u] = act(probs[:, u % 3, a:b], bank(3 * (u % 2), UB)[:, a:b], ACTF.Exp,
                                [s_done[u], pv_done.get(u - 3)], "exp")
            unit_free[u % 2] = [e_done[u]]

        def rests(u):
            for a, b in segments(u):
                r_done[u] = tt("dve", rest[:, u % 3, a:b], probs[:, u % 3, a:b], probs_h[:, u % 3, a:b, 1], ALU.subtract,
                               [e_done[u], pv_done.get(u - 3)], "rest")

        n_chunk = [0]
        chunk_of = {}
        pending = []

        def finish_chunk(now):
            h, c, acc, t_ev = now
            s = acc
            for k in range(TC):
                m = mm(bank(6 + acc)[:, k * VL:(k + 1) * VL], oT[:, s, k * P:(k + 1) * P], pick[:, :], k == 0, k == TC - 1,
                       [t_ev], "o_tm")
            acc_free[acc] = copy("dve", o_all[:, TC * c:TC * (c + 1), h, :],
                                 bank(6 + acc)[:, 0:TC * VL].rearrange("p (k c) -> p k c", k=TC), [m], "o_cp")

        def values(u):
            nonlocal fetched
            for i, (h, c, j, c0, w, col) in enumerate(units[u]):
                first = j == 0
                if first:
                    chunk_of[(h, c)] = n_chunk[0] % 2
                    n_chunk[0] += 1
                    while pending and pending[0][2] == chunk_of[(h, c)]:
                        finish_chunk(pending.pop(0))
                acc = chunk_of[(h, c)]
                last = seq_last[(h, c)] == (u, i)
                o = bank(6 + acc)
                mm(o[0:VW, c0:c0 + w], vhi[:, j, h, :], probs_h[:, u % 3, col:col + w, 1], first, False,
                   [r_done[u], acc_free[acc] if first else None, vlo_ready[h], v_ones])
                m = mm(o[0:VL, c0:c0 + w], vlo[:, h % 2, j, :], rest[:, u % 3, col:col + w], False, last, [],
                       "pv" if last or i == len(units[u]) - 1 else None)
                if last:
                    ev = act(oT[:, acc, :], o[0:VW, :], ACTF.Copy, [m, ("o_tm", pr.counts.get("o_tm", 0)) if "o_tm" in pr.counts else None], "o_ev")
                    pending.append((h, c, acc, ev))
                    if c == NC - 1:
                        op_free[h % 2] = [s_done[u]] if u + 1 not in s_done else [s_done[u + 1]]
                        vlo_free[h % 2] = m
                        if h + 2 < NH:
                            fetch(h + 2)
                            low_v(h + 2)
            pv_done[u] = m

        NU = len(units)
        scores(0)
        for u in range(NU):
            exps(u)
            rests(u)
            if u + 1 < NU:
                scores(u + 1)
            if u >= 1:
                values(u - 1)
                if len(pending) and pending[0][:2] not in [q[:2] for q in units[u - 1]]:
                    finish_chunk(pending.pop(0))
        values(NU - 1)
        while pending:
            finish_chunk(pending.pop(0))
        o_done = ("o_cp", pr.counts["o_cp"])
        for b in range(8):
            bank_free[b] = [e_done[NU - 1], e_done[NU - 2]][0] if b < 6 else acc_free[b - 6]

        x2 = []
        at_f, atT_f = [None, None], [None, None]
        den_free = None
        for g in range(NT // GT):
            n0 = g * GT
            dr = recip(den[:, :, :], o_all[:, n0:n0 + GT, :, VO], [o_done, den_free], "o_n")
            for n in range(n0, n0 + GT):
                s = n % 2
                a = tt("dve", at[:, s, :].rearrange("p (h c) -> p h c", c=HS), o_all[:, n, :, 0:HS],
                       den[:, n - n0, :].unsqueeze(2).broadcast_to([P, NH, HS]), ALU.mult, [dr, at_f[s]], "o_n")
                den_free = a
                b = 4 + s
                for ib in range(2):
                    t = tr(bank(b)[:, ib * P:(ib + 1) * P], at[:, s, ib * P:(ib + 1) * P], ident[:, :], [a, bank_free[b]], "o_tr")
                at_f[s] = t
                c = bank_free[b] = act(atT[:, s, :, :], bank(b)[:, 0:2 * P].rearrange("p (a t) -> p a t", a=2), ACTF.Copy, [t, atT_f[s]], "o_T")
                b = 6 + s
                for ib in range(2):
                    m = mm(bank(b)[:, 0:D], atT[:, s, ib, :], woT[:, ib, :], ib == 0, ib == 1, [c, bank_free[b]], "o_p")
                atT_f[s] = m
                a = bank_free[b] = tt("dve", x[:, n, :], bank(b)[:, 0:D], x[:, n, :], ALU.add, [m, x2_ready[n]], "o_x")
                x2.append(a)

        feed_forward(lambda n: x2[n], ffn_w, True)
        pr.wait("sp", ("out", pr.counts["out"]))

        block = ctx.enter_context(nc.Block())

        @block.sync
        def _(e):
            pr.emit("sp", e)

        @block.gpsimd
        def _(e):
            pr.emit("pool", e)

        @block.scalar
        def _(e):
            pr.emit("act", e)

        @block.vector
        def _(e):
            pr.emit("dve", e)

        @block.tensor
        def _(e):
            pr.emit("pe", e)


INPUTS = {
    "L0_attn_x": "x", "L0_attn_Wk": "Wk", "L0_attn_Wq": "Wq", "L0_attn_Wv": "Wv", "L0_attn_Wo": "Wo", "L0_attn_bo": "bo",
    "L0_attn_kln_g": "kln_g", "L0_attn_kln_b": "kln_b", "L0_attn_qln_g": "qln_g", "L0_attn_qln_b": "qln_b",
    "L0_ffn_base_W": "base_W", "L0_ffn_base_b": "base_b", "L0_ffn_shared_A": "shared_A", "L0_ffn_shared_B": "shared_B",
    "L0_ffn_routed_A": "routed_A", "L0_ffn_routed_B": "routed_B", "L0_ffn_router_W": "router_W", "L0_ffn_router_b": "router_b",
}


def kernel(**inputs):
    import numpy as np
    import concourse.bacc as bacc
    from concourse.bass_utils import run_bass_kernel_spmd

    nc = bacc.Bacc("TRN2", target_bir_lowering=False, num_devices=1)
    arrays, aps = {}, {}
    for name, short in INPUTS.items():
        a = np.ascontiguousarray(inputs[name])
        arrays[f"in_{short}"] = a
        aps[short] = nc.dram_tensor(f"in_{short}", a.shape, mybir.dt.from_np(a.dtype), kind="ExternalInput").ap()
    shape = tuple(inputs["L0_attn_x"].shape)
    out = nc.dram_tensor("out_x", shape, F32, kind="ExternalOutput").ap()
    build(nc, aps, out)
    r = run_bass_kernel_spmd(nc, [arrays], core_ids=[0])
    return r.results[0]["out_x"]
```

```python
import concourse.bass as bass
from concourse import mybir
from contextlib import ExitStack

F32 = mybir.dt.float32
F32R = mybir.dt.float32r
BF16 = mybir.dt.bfloat16
I32 = mybir.dt.int32
ALU = mybir.AluOpType
ACTF = mybir.ActivationFunctionType
AX = mybir.AxisListType


class Program:

    def __init__(self, nc, ctx):
        self.nc, self.ctx = nc, ctx
        self.queues = {"pe": [], "dve": [], "act": [], "pool": [], "sp": []}
        self.sems, self.counts, self.owner = {}, {}, {}
        self.waited = {e: {} for e in self.queues}

    def bump(self, name, by, eng):
        if name not in self.sems:
            self.sems[name] = self.ctx.enter_context(self.nc.semaphore(name))
            self.counts[name] = 0
            self.owner[name] = eng
        assert self.owner[name] == eng, name
        self.counts[name] += by
        return (name, self.counts[name])

    def wait(self, eng, *marks):
        for mark in marks:
            if mark is None:
                continue
            name, value = mark
            if self.waited[eng].get(name, 0) >= value:
                continue
            self.waited[eng][name] = value
            sem = self.sems[name]
            self.queues[eng].append(lambda e, sem=sem, value=value: e.wait_ge(sem, value))

    def do(self, eng, issue, after=(), says=None, by=1):
        self.wait(eng, *after)
        if says is None:
            self.queues[eng].append(issue)
            return None
        mark = self.bump(says, by, eng)
        sem = self.sems[says]
        self.queues[eng].append(lambda e: issue(e).then_inc(sem, by))
        return mark

    def dma(self, eng, out, in_, says, after=()):
        return self.do(eng, lambda e: e.dma_start(out, in_), after, says, 16)

    def only_if_zero(self, eng, flag):
        self.queues[eng].append(("if_zero", flag))
        self.saved = dict(self.saved) if hasattr(self, "saved") else {}
        self.saved[eng] = dict(self.waited[eng])

    def end_if(self, eng):
        self.queues[eng].append(("end", None))
        self.waited[eng] = self.saved[eng]

    def emit(self, eng, e):
        guard = None
        for item in self.queues[eng]:
            if isinstance(item, tuple):
                if item[0] == "if_zero":
                    flag = e.value_load(item[1], min_val=0, max_val=1)
                    guard = e.If(flag == 0)
                    guard.__enter__()
                else:
                    guard.__exit__(None, None, None)
            else:
                item(e)


def build(nc, ap, out, always_general=False):
    T, D = 4096, 256
    P = 128
    NT = T // P
    NH, HS = 16, 16
    NE, R = 6, 16
    NR = (NE + 1) * R
    NA = NR + NE
    EPS = 1e-5
    GT = 4
    CH = 512
    NC = T // CH
    TC = CH // P
    PARTS = 3
    Q_PARTS = [0, 0, 1, 1, 0, 2]
    K_PARTS = [0, 1, 0, 1, 2, 0]
    KR = len(Q_PARTS) * HS
    KS = KR + PARTS
    VO = HS
    VL = HS + 1
    VW = PARTS * VL
    UB = 3
    UW = UB * CH
    NEG = -1e30
    SAFE = 60.0
    SCALE = float(D) ** -0.25

    ctx = ExitStack()
    with ctx:
        pr = Program(nc, ctx)

        def sb(name, shape, dt=F32):
            return ctx.enter_context(nc.sbuf_tensor(name, shape, dt))

        def dram(name, shape, dt):
            return nc.dram_tensor(name, shape, dt, kind="Internal").ap()

        parts_d = dram("parts_d", [PARTS, 4, P, T], BF16)
        shift_d = dram("shift_d", [NH, PARTS, T], BF16)

        x = sb("x", [P, NT, D])
        wide = sb("wide", [P, 2, T])
        xnT = wide
        wide_b = wide[:, :, :].rearrange("p a t -> p (a t)").bitcast(BF16)
        ops = wide_b.rearrange("p (s a t) -> p s a t", s=2, a=2)
        ring = sb("ring", [P, 3 * UW])
        probs = ring[:, 0:3 * UW].rearrange("p (s c) -> p s c", s=3)
        rest = sb("rest", [P, 3, UW], BF16)
        HB = 120
        h_all = ring[:, 0:NT * HB].rearrange("p (n c) -> p n c", n=NT)
        big = sb("big", [P, NT * NH * VL])
        o_all = big[:, :].rearrange("p (n h c) -> p n h c", n=NT, h=NH)
        stage = big[:, 0:2 * PARTS * 4 * CH // 2].bitcast(BF16).rearrange(
            "p (s r b t) -> p s r b t", s=2, r=PARTS, b=4)
        vhi_f = sb("vhi", [P, NT * NH * VW], BF16)
        vhi = vhi_f[:, :].rearrange("p (n h c) -> p n h c", n=NT, h=NH)

        ident = sb("ident", [P, P])
        identb = sb("identb", [P, P], BF16)
        maskT = sb("maskT", [P, P], BF16)
        maskN = sb("maskN", [P, P], BF16)
        tri = sb("tri", [P, NE, NE])
        eps = sb("eps", [P, 1])
        wraw = vhi_f[:, 0:3 * 2 * D * 2].bitcast(F32).rearrange("p (s a d) -> p s a d", s=3, a=2)
        baseT = sb("baseT", [P, 2, D])
        aT = sb("aT", [P, 2, NA])
        bT = sb("bT", [NR + 1, D])
        WB = 2 * PARTS * 4 * CH // 2
        qkT = big[:, WB:WB + 4 * D].rearrange("p (a d) -> p a d", a=2)
        vT = big[:, WB + 4 * D:WB + 6 * D].rearrange("p (a d) -> p a d", a=2)
        woT = sb("woT", [P, 2, D])
        wmean = sb("wmean", [P, 2, 2 * NH])
        rb = sb("rb", [P, NE])
        bo = sb("bo", [P, D])
        gb = sb("gb", [P, 4])
        gbr = sb("gbr", [1, 4, HS])
        bound = sb("bound", [1, 16])
        flag = sb("flag", [1, 1], I32)
        st = sb("st", [P, NT, 6])
        mv = sb("mv", [P, NT, 2])
        rstd = sb("rstd", [P, NT])
        mix = sb("mix", [P, 2 * D + 2 * GT * NE * NE])
        xn = mix[:, 0:2 * D].rearrange("p (s d) -> p s d", s=2)
        gt, eq = (mix[:, 2 * D + i * GT * NE * NE:2 * D + (i + 1) * GT * NE * NE].rearrange(
            "p (n e f) -> p n e f", n=GT, e=NE) for i in range(2))
        lg = sb("lg", [P, GT, NE])
        ex = sb("ex", [P, GT, NE])
        r3 = sb("r3", [P, 4, GT])
        rank = sb("rank", [P, GT, NE])
        wt = sb("wt", [P, NT, NE + 1])
        hw = sb("hw", [P, 2, NR + 1])
        hT = sb("hT", [NR + 1, 2, P])
        sq = ring[:, 0:2 * CH].rearrange("p (s c) -> p s c", s=2)
        qn = ring[:, 2 * CH:4 * CH].rearrange("p (s c) -> p s c", s=2)
        qT = ring[:, 4 * CH:6 * CH].rearrange("p (s c) -> p s c", s=2)
        qr = ring[:, 6 * CH:8 * CH].rearrange("p (s c) -> p s c", s=2)
        vr = ring[:, 8 * CH:9 * CH].rearrange("p (s c) -> p s c", s=2)
        ss = sb("ss", [P, 2, 2 * NH])
        den = sb("den", [P, NT, NH])
        at = vhi_f[:, 0:2 * D * 2].bitcast(F32).rearrange("p (s d) -> p s d", s=2)
        atT = vhi_f[:, 2 * D * 2:4 * D * 2].bitcast(F32).rearrange("p (s a t) -> p s a t", s=2, a=2)
        mx2 = sb("mx2", [P, NT, 2])
        mx = sb("mx", [P, NT])
        mres = sb("mres", [P, 2, NT])
        mparts = sb("mparts", [P, PARTS, NT], BF16)
        mT = sb("mT", [PARTS * NT, P], BF16)

        ps = ctx.enter_context(nc.psum_tensor("ps", [P, 8 * CH], F32))

        def bank(b, n=1):
            return ps[:, b * CH:(b + n) * CH]

        bank_free = [None] * 8

        def mm(o, lhsT, rhs, start, stop, after=(), says=None):
            return pr.do("pe", lambda e: e.matmul(o, lhsT, rhs, start=start, stop=stop, skip_group_check=True), after, says)

        def tr(o, in_, idn, after=(), says=None):
            return pr.do("pe", lambda e: e.transpose(o, in_, idn), after, says)

        def act(o, in_, f, after=(), says=None, bias=0.0, scale=1.0):
            if f == ACTF.Copy:
                return pr.do("act", lambda e: e.activation(o, in_, f), after, says)
            return pr.do("act", lambda e: e.activation(o, in_, f, bias=bias, scale=scale), after, says)

        def tt(eng, o, a, b, op, after=(), says=None):
            return pr.do(eng, lambda e: e.tensor_tensor(o, a, b, op), after, says)

        def tsc(eng, o, a, s1, s2, op0, op1, after=(), says=None):
            if s2 is None:
                return pr.do(eng, lambda e: e.tensor_scalar(o, a, s1, None, op0), after, says)
            return pr.do(eng, lambda e: e.tensor_scalar(o, a, s1, s2, op0, op1), after, says)

        def stt(o, a, s, b, op0, op1, after=(), says=None):
            return pr.do("dve", lambda e: e.scalar_tensor_tensor(out=o, in0=a, scalar=s, in1=b, op0=op0, op1=op1), after, says)

        def red(o, a, op, after=(), says=None, absolute=False):
            if absolute:
                return pr.do("dve", lambda e: e.tensor_reduce(o, a, AX.X, op, apply_absolute_value=True), after, says)
            return pr.do("dve", lambda e: e.tensor_reduce(o, a, AX.X, op), after, says)

        def recip(o, a, after=(), says=None):
            return pr.do("dve", lambda e: e.reciprocal(o, a), after, says)

        def copy(eng, o, a, after=(), says=None):
            return pr.do(eng, lambda e: e.tensor_copy(o, a), after, says)

        def memset(eng, o, v, after=(), says=None):
            return pr.do(eng, lambda e: e.memset(o, v), after, says)

        def select(o, pattern, cm, base, op, fill, after=(), says=None):
            return pr.do("pool", lambda e: e.affine_select(out=o, in_=o, compare_op=op, fill=fill, base=base,
                                                           pattern=pattern, channel_multiplier=cm), after, says)

        z = memset("pool", ident[:, :], 0.0, says="const")
        ident_ok = select(ident[:, :], [[-1, P]], 1, 0, ALU.not_equal, 1.0, [z], "const")
        z = memset("pool", identb[:, :], 0.0, says="const")
        select(identb[:, :], [[-1, P]], 1, 0, ALU.not_equal, 1.0, [z], "const")
        z = memset("pool", maskT[:, :], 0.0, says="const")
        select(maskT[:, :], [[1, P]], -1, 0, ALU.is_ge, NEG, [z], "const")
        z = memset("pool", maskN[:, :], 0.0, says="const")
        select(maskN[:, :], [[-1, P]], 1, 0, ALU.is_ge, NEG, [z], "const")
        z = memset("pool", tri[:, :, :], 0.0, says="const")
        select(tri[:, :, :], [[-1, NE], [1, NE]], 0, 0, ALU.is_ge, 1.0, [z], "const")
        memset("pool", eps[:, :], EPS, says="const")
        memset("pool", wt[:, :, 0:1], 1.0, says="const")
        memset("pool", hw[:, :, NR:NR + 1], 1.0, says="const")
        const_ok = memset("pool", mT[:, :], 0.0, says="const")

        x_v = ap["x"][0].rearrange("(n p) d -> p n d", p=P)
        LT = 4
        x_in = []
        for i in range(NT // LT):
            x_in.append(pr.dma("sp", x[:, i * LT:(i + 1) * LT, :], x_v[:, i * LT:(i + 1) * LT, :], f"x_in{i}"))
        half = lambda w: w.rearrange("(b p) e -> p b e", p=P)
        A_RAW, B_RAW = 1, 2
        pr.dma("act", wraw[:, 0, :, :], half(ap["base_W"]), "w_base")
        w_base = ("w_base", 16)
        raw_a = wraw[:, A_RAW, 0, :]
        raw_b = wraw[:, B_RAW, :, 0:NR]
        pr.dma("act", raw_a[0:R, :], ap["shared_A"], "w_a")
        pr.dma("act", raw_a[R:NR, :], ap["routed_A"].rearrange("e r d -> (e r) d"), "w_a")
        w_a = pr.dma("act", raw_a[NR:NA, :], ap["router_W"], "w_a")
        pr.dma("act", raw_b[:, :, 0:R], ap["shared_B"].rearrange("(b p) r -> p b r", p=P), "w_b")
        for e_ in range(NE):
            w_b = pr.dma("act", raw_b[:, :, R + e_ * R:R + (e_ + 1) * R],
                         ap["routed_B"][e_].rearrange("(b p) r -> p b r", p=P), "w_b")
        w_bias = pr.dma("act", bT[NR:NR + 1, :], ap["base_b"].rearrange("(a n) -> a n", a=1), "w_bias")
        pr.dma("act", rb[:, :], ap["router_b"].partition_broadcast(P), "w_vec")
        w_vec = pr.dma("act", bo[:, :], ap["bo"].partition_broadcast(P), "w_vec")
        for i, name in enumerate(["qln_g", "qln_b", "kln_g", "kln_b"]):
            for h in range(P // HS):
                pr.dma("sp", gb[h * HS:(h + 1) * HS, i:i + 1], ap[name].rearrange("(a n) -> a n", n=1), "gb_in")
            gb_in = pr.dma("sp", gbr[:, i, :], ap[name].rearrange("(a n) -> a n", a=1), "gb_in")
        shift_zero = None
        for h in range(NH):
            shift_zero = pr.dma("sp", shift_d[h].rearrange("r (n t) -> (r n) t", t=P), mT[:, :], "shift_in", [const_ok])

        sc = pr.do("dve", lambda e: e.tensor_scalar_mul(gb[:, :], gb[:, :], SCALE), [gb_in], "bnd")
        red(bound[:, 0:4].unsqueeze(2), gbr[:, :, :], ALU.max, [gb_in], "bnd", absolute=True)
        b1 = red(bound[:, 0:4].unsqueeze(2), gbr[:, :, :], ALU.max, [("bnd", pr.counts["bnd"])], "bnd", absolute=True)
        b2 = tt("dve", gbr[:, :, :], gbr[:, :, :], gbr[:, :, :], ALU.mult, [b1], "bnd")
        b3 = red(bound[:, 4:8].unsqueeze(2), gbr[:, :, :], ALU.add, [b2], "bnd")
        b4 = act(bound[:, 8:12], bound[:, 4:8], ACTF.Sqrt, [b3], "bnd_sqrt")
        bv = bound[:, :].rearrange("a (k b c) -> a k b c", k=4, c=2)
        b5 = stt(bound[:, 12:14], bv[:, 0, :, 0], float(HS) ** 0.5, bv[:, 2, :, 1], ALU.mult, ALU.add, [b4], "bnd")
        b6 = tt("dve", bound[:, 14:15], bound[:, 12:13], bound[:, 13:14], ALU.mult, [b5], "bnd")
        limit = -1.0 if always_general else SAFE
        b7 = tsc("dve", bound[:, 15:16], bound[:, 14:15], SCALE * SCALE, limit, ALU.mult, ALU.is_le, [b6], "bnd")
        flag_ok = copy("dve", flag[:, :], bound[:, 15:16], [b7], "bnd")

        bank_turn = [0]

        def transpose_in(dst, src, rows, after, n_cols=P):
            b = bank_turn[0] % 4
            bank_turn[0] += 1
            t = tr(bank(b)[0:n_cols, 0:rows], src, ident[0:rows, 0:rows], list(after) + [bank_free[b]], "w_tr")
            bank_free[b] = copy("dve", dst, bank(b)[0:n_cols, 0:rows], [t], "w_cp")
            return bank_free[b]

        for ob in range(2):
            for ib in range(2):
                transpose_in(baseT[:, ib, ob * P:(ob + 1) * P], wraw[:, 0, ob, ib * P:(ib + 1) * P], P, [w_base, const_ok])
        for ib in range(2):
            transpose_in(aT[:, ib, :], raw_a[0:NA, ib * P:(ib + 1) * P], NA, [w_a])
        for ob in range(2):
            ffn_w = transpose_in(bT[0:NR, ob * P:(ob + 1) * P], raw_b[:, ob, :], P, [w_b], NR)
        pe_done = ("w_tr", pr.counts["w_tr"])

        def load_weight(slot, name, free, reload):
            return pr.dma("act", wraw[:, slot, :, :], half(ap[name]), f"w_in_{name}", [free])

        wq_in = load_weight(0, "Wq", pe_done, True)
        wk_in = load_weight(1, "Wk", pe_done, True)
        wv_in = load_weight(2, "Wv", pe_done, True)

        def attention_weights():
            for slot, dst, off, ready in ((0, qkT, 0, wq_in), (1, qkT, D, wk_in), (2, vT, 0, wv_in)):
                for ob in range(2):
                    for ib in range(2):
                        m = transpose_in(dst[:, ib, off + ob * P:off + (ob + 1) * P],
                                         wraw[:, slot, ob, ib * P:(ib + 1) * P], P, [ready])
            used = ("w_tr", pr.counts["w_tr"])
            wo_in = load_weight(0, "Wo", used, True)
            for ob in range(2):
                for ib in range(2):
                    m = transpose_in(woT[:, ib, ob * P:(ob + 1) * P], wraw[:, 0, ob, ib * P:(ib + 1) * P], P, [wo_in])
            a1 = red(wmean[:, :, :].rearrange("p a (h c) -> p (a h) c", c=1), qkT[:, :, :].rearrange("p a (h c) -> p (a h) c", c=HS), ALU.add, [m], "w_mean")
            a2 = pr.do("dve", lambda e: e.tensor_scalar_mul(wmean[:, :, :], wmean[:, :, :], 1.0 / HS), [a1], "w_mean")
            for ib in range(2):
                a3 = tt("dve", qkT[:, ib, :].rearrange("p (h c) -> p h c", c=HS), qkT[:, ib, :].rearrange("p (h c) -> p h c", c=HS),
                        wmean[:, ib, :].unsqueeze(2).broadcast_to([P, 2 * NH, HS]), ALU.subtract, [a2], "w_mean")
            return a3

        def skewed(items, stages):
            for t in range(len(items) + len(stages) - 1):
                for k in reversed(range(len(stages))):
                    if 0 <= t - k < len(items):
                        stages[k](items[t - k])
                yield

        def together(*streams):
            streams = [q for q in streams if q is not None]
            while streams:
                for q in list(streams):
                    try:
                        next(q)
                    except StopIteration:
                        streams.remove(q)

        NG = NT // GT
        group = lambda g: list(range(g * GT, (g + 1) * GT))
        rstd_ok = {}

        def stats(g, ready):
            n0, n1 = g * GT, (g + 1) * GT
            for n in range(n0, n1):
                s = pr.do("dve", lambda e, n=n: e.bn_stats(st[:, n, :], x[:, n, :]), [ready(n)], "ln_st")
                yield
            for n in range(n0, n1):
                s2 = pr.do("dve", lambda e, n=n: e.bn_aggr(mv[:, n, :], st[:, n, :]), [s], "ln_st")
            s3 = act(rstd[:, n0:n1], mv[:, n0:n1, 1], ACTF.Sqrt, [s2], "ln_sqrt", bias=eps[:, :])
            yield
            rstd_ok[g] = recip(rstd[:, n0:n1], rstd[:, n0:n1], [s3], "ln_r")

        xn_free = [None, None]
        xn_ok, xnT_ok = {}, {}

        def scale_tile(n):
            s = n % 2
            xn_ok[n] = tsc("dve", xn[:, s, :], x[:, n, :], mv[:, n, 0:1], rstd[:, n:n + 1], ALU.subtract, ALU.mult,
                           [rstd_ok[n // GT], xn_free[s]], "xn")

        def turn_tile(n):
            s = n % 2
            for ib in range(2):
                t = tr(bank(s)[:, ib * P:(ib + 1) * P], xn[:, s, ib * P:(ib + 1) * P], ident[:, :], [xn_ok[n], bank_free[s]], "xn_tr")
            xn_free[s] = t
            xnT_ok[n] = bank_free[s] = act(xnT[:, :, n * P:(n + 1) * P], bank(s)[:, 0:2 * P].rearrange("p (a t) -> p a t", a=2),
                                           ACTF.Copy, [t], "xnT")

        out_v = out[0].rearrange("(n p) d -> p n d", p=P)

        def feed_forward(ready, after_weights, final, before=None):
            done = {}
            h_ok, wts, hw_ok, hT_ok = {}, {}, {}, {}
            hw_free, hT_free = [None, None], [None, None]

            def inner_a(n):
                for ib in range(2):
                    m = mm(bank(2)[:, 0:NA], xnT[:, ib, n * P:(n + 1) * P], aT[:, ib, :], ib == 0, ib == 1,
                           [xnT_ok[n], after_weights, bank_free[2]], "ff_a")
                h_ok[n] = bank_free[2] = act(h_all[:, n, 0:NA], bank(2)[:, 0:NA], ACTF.Copy, [m], "ff_h")

            def route(g):
                n0 = g * GT
                tiles = slice(n0, n0 + GT)
                a = tt("dve", lg[:, :, :], h_all[:, tiles, NR:NA], rb[:, :].unsqueeze(1).broadcast_to([P, GT, NE]), ALU.add, [h_ok[n0 + GT - 1], w_vec], "rt")
                yield
                a = red(r3[:, 0, :].unsqueeze(2), lg[:, :, :], ALU.max, [a], "rt")
                yield
                a = tt("dve", lg[:, :, :], lg[:, :, :], r3[:, 0, :].unsqueeze(2).broadcast_to([P, GT, NE]), ALU.subtract, [a], "rt")
                a = act(ex[:, :, :], lg[:, :, :], ACTF.Exp, [a], "rt_exp")
                yield
                red(r3[:, 1, :].unsqueeze(2), ex[:, :, :], ALU.add, [a], "rt")
                other = ex[:, :, :].unsqueeze(2).broadcast_to([P, GT, NE, NE])
                own = ex[:, :, :].unsqueeze(3).broadcast_to([P, GT, NE, NE])
                tt("dve", gt[:, :, :, :], other, own, ALU.is_gt, [a], "rt")
                a = tt("dve", eq[:, :, :, :], other, own, ALU.is_equal, [a], "rt")
                yield
                a = tt("dve", eq[:, :, :, :], eq[:, :, :, :], tri[:, :, :].unsqueeze(1).broadcast_to([P, GT, NE, NE]), ALU.mult, [a, const_ok], "rt")
                yield
                a = tt("dve", gt[:, :, :, :], gt[:, :, :, :], eq[:, :, :, :], ALU.add, [a], "rt")
                yield
                a = red(rank[:, :, :].unsqueeze(3), gt[:, :, :, :], ALU.add, [a], "rt")
                yield
                a = stt(rank[:, :, :], rank[:, :, :], 2.0, ex[:, :, :], ALU.is_lt, ALU.mult, [a], "rt")
                a = red(r3[:, 2, :].unsqueeze(2), rank[:, :, :], ALU.add, [a], "rt")
                yield
                a = stt(r3[:, 3, :], r3[:, 1, :], 1e-6, r3[:, 2, :], ALU.mult, ALU.add, [a], "rt")
                a = recip(r3[:, 3, :], r3[:, 3, :], [a], "rt")
                yield
                wts[g] = tt("dve", wt[:, tiles, 1:NE + 1], rank[:, :, :], r3[:, 3, :].unsqueeze(2).broadcast_to([P, GT, NE]), ALU.mult, [a], "rt")

            def weigh(n):
                s = n % 2
                hw_ok[n] = tt("dve", hw[:, s, 0:NR].rearrange("p (e r) -> p e r", r=R), h_all[:, n, 0:NR].rearrange("p (e r) -> p e r", r=R),
                              wt[:, n, :].unsqueeze(2).broadcast_to([P, NE + 1, R]), ALU.mult, [wts[n // GT], hw_free[s]], "ff_w")

            def turn_inner(n):
                s = n % 2
                hw_free[s] = t = tr(bank(3)[0:NR + 1, 0:P], hw[:, s, :], ident[:, :], [hw_ok[n], bank_free[3]], "ff_tr")
                hT_ok[n] = bank_free[3] = act(hT[:, s, :], bank(3)[0:NR + 1, 0:P], ACTF.Copy, [t, hT_free[s]], "ff_hT")

            def outer(n):
                s = n % 2
                b = 4 + s
                mm(bank(b)[:, 0:D], xnT[:, 0, n * P:(n + 1) * P], baseT[:, 0, :], True, False, [bank_free[b]])
                mm(bank(b)[:, 0:D], xnT[:, 1, n * P:(n + 1) * P], baseT[:, 1, :], False, False)
                m = hT_free[s] = mm(bank(b)[:, 0:D], hT[:, s, :], bT[:, :], False, True, [hT_ok[n], w_bias], "ff_o")
                done[n] = bank_free[b] = stt(x[:, n, :], bank(b)[:, 0:D], 0.5, x[:, n, :], ALU.mult, ALU.add, [m], "ff_x")
                if final and n % 2 == 1:
                    pr.dma("sp", out_v[:, n - 1:n + 1, :], x[:, n - 1:n + 1, :], "out", [done[n]])

            lag = 0 if before is None else 1
            for t in range(NG + 3 + lag):
                part = lambda g, make: make(g) if 0 <= g < NG else None
                together(part(t - 3 - lag, lambda g: skewed(group(g), [weigh, turn_inner, outer])),
                         part(t - 2 - lag, route),
                         part(t - 1 - lag, lambda g: skewed(group(g), [scale_tile, turn_tile, inner_a])),
                         part(t - lag, lambda g: stats(g, ready)),
                         part(t, before) if before is not None else None)
            return done

        x1 = feed_forward(lambda n: x_in[n // LT], ffn_w, False)
        w_centred = attention_weights()
        weights_used = ("w_tr", pr.counts["w_tr"])
        memset("pool", vhi[:, :, :, VO:VO + 1], 1.0, [weights_used], "v_ones")
        for r_ in range(1, PARTS):
            v_ones = memset("pool", vhi[:, :, :, r_ * VL + HS:(r_ + 1) * VL], 0.0, [], "v_ones")

        stage_free = [None, None]
        sq_f, qn_f, qT_f, qr_f, vr_f, ss_f = ([None, None] for _ in range(6))
        ss_ok, qn_ok, qT_ok, qr_ok, vr_ok = {}, {}, {}, {}, {}
        heads = lambda t_: t_.rearrange("p (h c) -> p h c", c=HS)

        def project_qkv(n):
            s = n % 2
            b = 2 + s
            for ib in range(2):
                m = mm(bank(b), xnT[:, ib, n * P:(n + 1) * P], qkT[:, ib, :], ib == 0, ib == 1, [xnT_ok[n], w_centred, bank_free[b]], "qk")
            for ib in range(2):
                mv_ = mm(bank(4 + s)[:, 0:D], xnT[:, ib, n * P:(n + 1) * P], vT[:, ib, :], ib == 0, ib == 1, [bank_free[4 + s]], "v")
            a = act(sq[:, s, :], bank(b), ACTF.Square, [m, sq_f[s]], "qk_sq")
            ss_ok[n] = sq_f[s] = red(ss[:, s, :].unsqueeze(2), heads(sq[:, s, :]), ALU.add, [a, ss_f[s]], "qk_ss")
            v0 = heads(bank(4 + s)[:, 0:D])
            a = act(vhi[:, n, :, 0:HS], v0, ACTF.Copy, [mv_, v_ones], "vcut_a")
            vr_ok[n] = bank_free[4 + s] = tt("dve", heads(vr[:, s, :]), v0, vhi[:, n, :, 0:HS], ALU.subtract, [a, vr_f[s]], "vcut_d")

        def scale_heads(n):
            s = n % 2
            b = 2 + s
            a = act(ss[:, s, :], ss[:, s, :], ACTF.Sqrt, [ss_ok[n]], "qk_rt", bias=eps[:, :], scale=1.0 / HS)
            a = recip(ss[:, s, :], ss[:, s, :], [a], "qk_ss")
            qn_ok[n] = bank_free[b] = ss_f[s] = tt("dve", heads(qn[:, s, :]), heads(bank(b)), ss[:, s, :].unsqueeze(2).broadcast_to([P, 2 * NH, HS]),
                                                   ALU.mult, [a, qn_f[s]], "qk_n")

        def turn_heads(n):
            s = n % 2
            b = 6 + s
            for k in range(4):
                t = tr(bank(b)[:, k * P:(k + 1) * P], qn[:, s, k * P:(k + 1) * P], ident[:, :], [qn_ok[n], bank_free[b]], "qk_tr")
            qn_f[s] = t
            tsc("dve", qT[:, s, 0:2 * P], bank(b)[:, 0:2 * P], gb[:, 0:1], gb[:, 1:2], ALU.mult, ALU.add, [t, qT_f[s], sc], "qk_T")
            qT_ok[n] = bank_free[b] = tsc("dve", qT[:, s, 2 * P:], bank(b)[:, 2 * P:], gb[:, 2:3], gb[:, 3:4], ALU.mult, ALU.add, [t], "qk_T")
            a = act(vhi[:, n, :, VL:VL + HS], heads(vr[:, s, :]), ACTF.Copy, [vr_ok[n]], "vcut_a")
            vr_f[s] = tt("pool", vhi[:, n, :, 2 * VL:2 * VL + HS], heads(vr[:, s, :]), vhi[:, n, :, VL:VL + HS], ALU.subtract, [a], "vcut_p")

        def staged(n, i):
            return stage[:, (n // TC) % 2, i, :, (n % TC) * P:(n % TC + 1) * P]

        def cut_first(n):
            s = n % 2
            full = qT[:, s, :].rearrange("p (b t) -> p b t", b=4)
            left = qr[:, s, :].rearrange("p (b t) -> p b t", b=4)
            a = act(staged(n, 0), full, ACTF.Copy, [qT_ok[n], stage_free[(n // TC) % 2]], "cut_a")
            qr_ok[n] = qT_f[s] = tt("pool", left, full, staged(n, 0), ALU.subtract, [a, qr_f[s]], "cut_p")

        def cut_rest(n):
            s, sg = n % 2, (n // TC) % 2
            left = qr[:, s, :].rearrange("p (b t) -> p b t", b=4)
            a = act(staged(n, 1), left, ACTF.Copy, [qr_ok[n]], "cut_a")
            a = qr_f[s] = tt("pool", staged(n, 2), left, staged(n, 1), ALU.subtract, [a], "cut_p")
            if n % TC == TC - 1:
                c0 = (n // TC) * CH
                for i in range(PARTS):
                    stage_free[sg] = pr.dma("sp", parts_d[i, :, :, c0:c0 + CH].rearrange("b p t -> p b t"), stage[:, sg, i, :, :],
                                            f"parts{sg}", [a])

        qkv = skewed(list(range(NT)), [scale_tile, turn_tile, project_qkv, scale_heads, turn_heads, cut_first, cut_rest])

        def all_stats():
            for g in range(1, NG):
                for _ in stats(g, lambda n: x1[n]):
                    yield

        for _ in stats(0, lambda n: x1[n]):
            pass
        ahead = all_stats()
        for _ in range(3):
            next(ahead)
        together(ahead, ahead, qkv)
        a = ("vcut_p", pr.counts["vcut_p"])
        v_done = a
        x2_ready = [pr.do("pool", lambda e, n=n: e.tensor_tensor(x[:, n, :], x[:, n, :], bo[:, :], ALU.add), [x1[n], rstd_ok[NG - 1], w_vec, xn_free[0], xn_free[1]], "x_bo") for n in range(NT)]
        prep_pe = [("qk", pr.counts["qk"]), ("v", pr.counts["v"])]
        parts_all = [stage_free[0], stage_free[1]]

        def load_operands(h, slot, rows, sem, after):
            blk, row = h // 8, (h % 8) * HS
            for i, (a_, b_) in enumerate(zip(Q_PARTS, K_PARTS)):
                pr.dma("sp", ops[i * HS:(i + 1) * HS, slot, 0, :], parts_d[a_, blk, row:row + HS, :], sem, after)
                mk = pr.dma("sp", ops[i * HS:(i + 1) * HS, slot, 1, :], parts_d[b_, 2 + blk, row:row + HS, :], sem, after)
            if rows == KS:
                mk = pr.dma("sp", ops[KR:KS, slot, 0, :], shift_d[h], sem, after)
            return mk

        engines = ["pe", "dve", "sp"]
        for e_ in engines:
            pr.wait(e_, flag_ok)
            pr.only_if_zero(e_, flag[0:1, 0:1])
        slot_free = [None, None]
        reg_free = [[bank_free[i] for i in range(4)], [bank_free[i] for i in range(4, 8)]]
        turn = 0
        mT_free = shift_zero
        mp_free = None
        for h in range(NH):
            s = h % 2
            ready = load_operands(h, s, KR, f"gen_in{s}", parts_all + prep_pe + [slot_free[s]])
            last = None
            for n in range(NT):
                width = (n + 1) * P
                for k, j0 in enumerate(range(0, width, 4 * CH)):
                    w = min(4 * CH, width - j0)
                    region = bank(4 * (turn % 2), 4)
                    for c0 in range(0, w, CH):
                        cw = min(CH, w - c0)
                        diag = j0 + c0 + cw == width
                        m = mm(region[:, c0:c0 + cw], ops[0:KR, s, 0, n * P:(n + 1) * P], ops[0:KR, s, 1, j0 + c0:j0 + c0 + cw],
                               True, not diag, [ready] + reg_free[turn % 2], None if diag else "gen_mm")
                        if diag:
                            m = mm(region[:, c0 + cw - P:c0 + cw], identb[:, :], maskN[:, :], False, True, [], "gen_mm")
                    last = red(mx2[:, n, k:k + 1], region[:, 0:w], ALU.max, [m, mp_free], "gen_max")
                    reg_free[turn % 2] = [last]
                    turn += 1
            slot_free[s] = m
            two = NT // 2
            copy("dve", mx[:, 0:two], mx2[:, 0:two, 0], [last], "gen_v")
            a = tt("dve", mx[:, two:], mx2[:, two:, 0], mx2[:, two:, 1], ALU.max, [last], "gen_v")
            a = tsc("dve", mres[:, 0, :], mx[:, :], -1.0, None, ALU.mult, None, [a], "gen_v")
            a = copy("dve", mparts[:, 0, :], mres[:, 0, :], [a], "gen_v")
            a = tt("dve", mres[:, 1, :], mres[:, 0, :], mparts[:, 0, :], ALU.subtract, [a], "gen_v")
            a = copy("dve", mparts[:, 1, :], mres[:, 1, :], [a], "gen_v")
            a = tt("dve", mparts[:, 2, :], mres[:, 1, :], mparts[:, 1, :], ALU.subtract, [a], "gen_v")
            mp_free = a
            b = 4 * (turn % 2)
            t = tr(bank(b)[0:PARTS * NT, 0:P // 2].bitcast(BF16), mparts[:, :, :].rearrange("p r n -> p (r n)"), identb[:, :],
                   [a] + reg_free[turn % 2], "gen_tr")
            a = copy("dve", mT[:, :], bank(b)[0:PARTS * NT, 0:P // 2].bitcast(BF16), [t, mT_free], "gen_v")
            reg_free[turn % 2] = [a]
            turn += 1
            mT_free = pr.dma("sp", shift_d[h].rearrange("r (n t) -> (r n) t", t=P), mT[:, :], "gen_out", [a])
        pr.wait("sp", mT_free)
        pr.wait("pe", *reg_free[0], *reg_free[1])
        gen_last_mm = None
        for e_ in engines:
            pr.end_if(e_)

        units, banks = [], []
        chunk_last = {}
        for h in range(NH):
            for c in range(NC):
                base = TC * c
                rows = [[(j, 0, CH, 0)] for j in range(base + 1)]
                rows.append([(base + 1, P, CH - P, 0), (base + 3, 3 * P, P, CH - P)])
                rows.append([(base + 2, 2 * P, 2 * P, 0)])
                for r_ in rows:
                    banks.append([(h, c) + q for q in r_])
        for i in range(0, len(banks), UB):
            units.append([(q[:5] + (k * CH + q[5],)) for k, bk in enumerate(banks[i:i + UB]) for q in bk])
        seq_last = {}
        for u, un in enumerate(units):
            for i, q in enumerate(un):
                seq_last[(q[0], q[1])] = (u, i)

        ones_rows = memset("dve", ops[KR:KS, :, 1, :], 1.0, [("xnT", pr.counts["xnT"])] + prep_pe, "ones")
        op_ready = {}
        op_free = [prep_pe, prep_pe]

        def fetch(h):
            op_ready[h] = load_operands(h, h % 2, KS, f"op_in{h % 2}", parts_all + [shift_zero] + list(op_free[h % 2]))

        for h in range(2):
            fetch(h)
        unit_free = [[bank_free[i] for i in range(3)], [bank_free[i] for i in range(3, 6)]]
        acc_free = [bank_free[6], bank_free[7]]
        s_done, e_done, r_done, pv_done = {}, {}, {}, {}
        fetched = 2
        probs_h = ring[:, 0:3 * UW].bitcast(BF16).rearrange("p (s c two) -> p s c two", s=3, two=2)

        def scores(u):
            for i, (h, c, j, c0, w, col) in enumerate(units[u]):
                o = bank(3 * (u % 2), UB)[:, col:col + w]
                diag = j >= TC * c
                last_in = i == len(units[u]) - 1
                q0 = c * CH + c0
                m = mm(o, ops[0:KS, h % 2, 1, j * P:(j + 1) * P], ops[0:KS, h % 2, 0, q0:q0 + w],
                       col % CH == 0, not diag, [op_ready[h], ones_rows] + unit_free[u % 2], None if diag or not last_in else "s")
                if diag:
                    m = mm(o[:, 0:P], identb[:, :], maskT[:, :], False, True, [], "s" if last_in else None)
            s_done[u] = m

        def segments(u):
            segs = []
            for (_, _, _, _, w, col) in units[u]:
                if segs and segs[-1][1] == col:
                    segs[-1][1] = col + w
                else:
                    segs.append([col, col + w])
            return segs

        def exps(u):
            for a, b in segments(u):
                e_done[u] = act(probs[:, u % 3, a:b], bank(3 * (u % 2), UB)[:, a:b], ACTF.Exp,
                                [s_done[u], pv_done.get(u - 3)], "exp")
            unit_free[u % 2] = [e_done[u]]

        def rests(u):
            for a, b in segments(u):
                r_done[u] = tt("dve", rest[:, u % 3, a:b], probs[:, u % 3, a:b], probs_h[:, u % 3, a:b, 1], ALU.subtract,
                               [e_done[u], pv_done.get(u - 3)], "rest")

        n_chunk = [0]
        chunk_of = {}
        pending = []

        def finish_chunk(h, c, acc, complete):
            parts = bank(6 + acc)[:, 0:TC * VW].rearrange("p (k r c) -> p k c r", k=TC, r=PARTS)
            acc_free[acc] = pr.do("dve", lambda e: e.tensor_reduce(
                o_all[:, TC * c:TC * (c + 1), h, :].unsqueeze(3), parts, AX.X, ALU.add), [complete], "o_cp")

        def values(u):
            for i, (h, c, j, c0, w, col) in enumerate(units[u]):
                first = j == 0
                if first:
                    chunk_of[(h, c)] = n_chunk[0] % 2
                    n_chunk[0] += 1
                    while pending and pending[0][2] == chunk_of[(h, c)]:
                        finish_chunk(*pending.pop(0))
                acc = chunk_of[(h, c)]
                last = seq_last[(h, c)] == (u, i)
                for k in range(w // P):
                    tile = c0 // P + k
                    o = bank(6 + acc)[:, tile * VW:(tile + 1) * VW]
                    cols = slice(col + k * P, col + (k + 1) * P)
                    ends = k == w // P - 1
                    mm(o, probs_h[:, u % 3, cols, 1], vhi[:, j, h, :], first and k == 0, False,
                       [r_done[u], acc_free[acc] if first else None])
                    m = mm(o, rest[:, u % 3, cols], vhi[:, j, h, :], False, last and ends, [],
                           "pv" if ends and (last or i == len(units[u]) - 1) else None)
                if last:
                    pending.append((h, c, acc, m))
                    if c == NC - 1:
                        op_free[h % 2] = [s_done[u]] if u + 1 not in s_done else [s_done[u + 1]]
                        if h + 2 < NH:
                            fetch(h + 2)
            pv_done[u] = m

        NU = len(units)
        scores(0)
        for u in range(NU):
            exps(u)
            rests(u)
            if pending and u >= 2:
                finish_chunk(*pending.pop(0))
            if u + 1 < NU:
                scores(u + 1)
            if u >= 1:
                values(u - 1)
        values(NU - 1)
        while pending:
            finish_chunk(*pending.pop(0))
        o_done = ("o_cp", pr.counts["o_cp"])
        for b in range(8):
            bank_free[b] = e_done[NU - 1] if b < 6 else acc_free[b - 6]

        x2, at_ok, atT_ok = {}, {}, {}
        at_f, atT_f = [None, None], [None, None]
        den_ok = recip(den[:, :, :], o_all[:, :, :, VO], [o_done], "o_n")

        def over_sum(n):
            s = n % 2
            at_ok[n] = tt("dve", heads(at[:, s, :]), o_all[:, n, :, 0:HS],
                          den[:, n, :].unsqueeze(2).broadcast_to([P, NH, HS]), ALU.mult, [den_ok, at_f[s]], "o_n")

        def turn_out(n):
            s = n % 2
            for ib in range(2):
                t = tr(bank(6)[:, ib * P:(ib + 1) * P], at[:, s, ib * P:(ib + 1) * P], ident[:, :], [at_ok[n], bank_free[6]], "o_tr")
            at_f[s] = t
            atT_ok[n] = bank_free[6] = act(atT[:, s, :, :], bank(6)[:, 0:2 * P].rearrange("p (a t) -> p a t", a=2), ACTF.Copy, [t, atT_f[s]], "o_T")

        def project_out(n):
            s = n % 2
            for ib in range(2):
                m = mm(bank(7)[:, 0:D], atT[:, s, ib, :], woT[:, ib, :], ib == 0, ib == 1, [atT_ok[n], bank_free[7]], "o_p")
            atT_f[s] = m
            x2[n] = bank_free[7] = tt("dve", x[:, n, :], bank(7)[:, 0:D], x[:, n, :], ALU.add, [m, x2_ready[n]], "o_x")

        feed_forward(lambda n: x2[n], ffn_w, True, before=lambda g: skewed(group(g), [over_sum, turn_out, project_out]))
        pr.wait("sp", ("out", pr.counts["out"]))

        block = ctx.enter_context(nc.Block())

        @block.sync
        def _(e):
            pr.emit("sp", e)

        @block.gpsimd
        def _(e):
            pr.emit("pool", e)

        @block.scalar
        def _(e):
            pr.emit("act", e)

        @block.vector
        def _(e):
            pr.emit("dve", e)

        @block.tensor
        def _(e):
            pr.emit("pe", e)


INPUTS = {
    "L0_attn_x": "x", "L0_attn_Wk": "Wk", "L0_attn_Wq": "Wq", "L0_attn_Wv": "Wv", "L0_attn_Wo": "Wo", "L0_attn_bo": "bo",
    "L0_attn_kln_g": "kln_g", "L0_attn_kln_b": "kln_b", "L0_attn_qln_g": "qln_g", "L0_attn_qln_b": "qln_b",
    "L0_ffn_base_W": "base_W", "L0_ffn_base_b": "base_b", "L0_ffn_shared_A": "shared_A", "L0_ffn_shared_B": "shared_B",
    "L0_ffn_routed_A": "routed_A", "L0_ffn_routed_B": "routed_B", "L0_ffn_router_W": "router_W", "L0_ffn_router_b": "router_b",
}


def kernel(**inputs):
    import numpy as np
    import concourse.bacc as bacc
    from concourse.bass_utils import run_bass_kernel_spmd

    nc = bacc.Bacc("TRN2", target_bir_lowering=False, num_devices=1)
    arrays, aps = {}, {}
    for name, short in INPUTS.items():
        a = np.ascontiguousarray(inputs[name])
        arrays[f"in_{short}"] = a
        aps[short] = nc.dram_tensor(f"in_{short}", a.shape, mybir.dt.from_np(a.dtype), kind="ExternalInput").ap()
    shape = tuple(inputs["L0_attn_x"].shape)
    out = nc.dram_tensor("out_x", shape, F32, kind="ExternalOutput").ap()
    build(nc, aps, out)
    r = run_bass_kernel_spmd(nc, [arrays], core_ids=[0])
    return r.results[0]["out_x"]
```

```python
import concourse.bass as bass
from concourse import mybir
from contextlib import ExitStack

F32 = mybir.dt.float32
BF16 = mybir.dt.bfloat16
I32 = mybir.dt.int32
ALU = mybir.AluOpType
ACTF = mybir.ActivationFunctionType
AX = mybir.AxisListType


class Program:

    def __init__(self, nc, ctx):
        self.nc, self.ctx = nc, ctx
        self.queues = {"pe": [], "dve": [], "act": [], "pool": [], "sp": []}
        self.sems, self.counts, self.owner = {}, {}, {}
        self.waited = {e: {} for e in self.queues}
        self.saved = {}

    def bump(self, name, by, eng):
        if name not in self.sems:
            self.sems[name] = self.ctx.enter_context(self.nc.semaphore(name))
            self.counts[name] = 0
            self.owner[name] = eng
        assert self.owner[name] == eng, name
        self.counts[name] += by
        return (name, self.counts[name])

    def wait(self, eng, *marks):
        for mark in marks:
            if mark is None:
                continue
            name, value = mark
            if self.waited[eng].get(name, 0) >= value:
                continue
            self.waited[eng][name] = value
            sem = self.sems[name]
            self.queues[eng].append(lambda e, sem=sem, value=value: e.wait_ge(sem, value))

    def do(self, eng, issue, after=(), says=None, by=1):
        self.wait(eng, *after)
        if says is None:
            self.queues[eng].append(issue)
            return None
        mark = self.bump(says, by, eng)
        sem = self.sems[says]
        self.queues[eng].append(lambda e: issue(e).then_inc(sem, by))
        return mark

    def dma(self, eng, out, in_, says, after=()):
        return self.do(eng, lambda e: e.dma_start(out, in_), after, says, 16)

    def only_if_zero(self, eng, flag):
        self.queues[eng].append(("if_zero", flag))
        self.saved[eng] = dict(self.waited[eng])

    def end_if(self, eng):
        self.queues[eng].append(("end", None))
        self.waited[eng] = self.saved[eng]

    def emit(self, eng, e):
        guard = None
        for item in self.queues[eng]:
            if isinstance(item, tuple):
                if item[0] == "if_zero":
                    flag = e.value_load(item[1], min_val=0, max_val=1)
                    guard = e.If(flag == 0)
                    guard.__enter__()
                else:
                    guard.__exit__(None, None, None)
            else:
                item(e)


def build(nc, ap, out, always_general=False):
    T, D = 4096, 256
    P = 128
    NT = T // P
    NH, HS = 16, 16
    NE, R = 6, 16
    NR = (NE + 1) * R
    NA = NR + NE
    EPS = 1e-5
    GT = 4
    CH = 512
    NC = T // CH
    TC = CH // P
    PARTS = 3
    Q_PARTS = [0, 0, 1, 1, 0, 2]
    K_PARTS = [0, 1, 0, 1, 2, 0]
    KR = len(Q_PARTS) * HS
    KS = KR + PARTS
    VO = HS
    VL = HS + 1
    VW = PARTS * VL
    UB = 3
    UW = UB * CH
    NEG = -1e30
    SAFE = 60.0
    SCALE = float(D) ** -0.25

    ctx = ExitStack()
    with ctx:
        pr = Program(nc, ctx)

        def sb(name, shape, dt=F32):
            return ctx.enter_context(nc.sbuf_tensor(name, shape, dt))

        def dram(name, shape, dt):
            return nc.dram_tensor(name, shape, dt, kind="Internal").ap()

        parts_d = dram("parts_d", [PARTS, 4, P, T], BF16)
        shift_d = dram("shift_d", [NH, PARTS, T], BF16)

        x = sb("x", [P, NT, D])
        wide = sb("wide", [P, 2, T])
        xnT = wide
        ops = wide[:, :, :].rearrange("p a t -> p (a t)").bitcast(BF16).rearrange(
            "p (s a t) -> p s a t", s=2, a=2)
        ring = sb("ring", [P, 3 * UW])
        probs = ring[:, 0:3 * UW].rearrange("p (s c) -> p s c", s=3)
        halves = ring[:, 0:3 * UW].bitcast(BF16).rearrange("p (s c two) -> p s c two", s=3, two=2)
        rest = sb("rest", [P, 3, UW], BF16)
        HB = 120
        h_all = ring[:, 0:NT * HB].rearrange("p (n c) -> p n c", n=NT)
        big = sb("big", [P, NT * NH * VL])
        o_all = big[:, :].rearrange("p (n h c) -> p n h c", n=NT, h=NH)
        stage = big[:, 0:2 * PARTS * 4 * CH // 2].bitcast(BF16).rearrange(
            "p (s r b t) -> p s r b t", s=2, r=PARTS, b=4)
        vhi_f = sb("vhi", [P, NT * NH * VW], BF16)
        vhi = vhi_f[:, :].rearrange("p (n h c) -> p n h c", n=NT, h=NH)

        ident = sb("ident", [P, P])
        identb = sb("identb", [P, P], BF16)
        maskT = sb("maskT", [P, P], BF16)
        maskN = sb("maskN", [P, P], BF16)
        tri = sb("tri", [P, NE, NE])
        eps = sb("eps", [P, 1])
        wraw = vhi_f[:, 0:7 * 2 * D * 2].bitcast(F32).rearrange("p (s a d) -> p s a d", s=7, a=2)
        baseT = sb("baseT", [P, 2, D])
        aT = sb("aT", [P, 2, NA])
        bT = sb("bT", [NR + 1, D])
        WB = 2 * PARTS * 4 * CH // 2
        qkT = big[:, WB:WB + 4 * D].rearrange("p (a d) -> p a d", a=2)
        vT = big[:, WB + 4 * D:WB + 6 * D].rearrange("p (a d) -> p a d", a=2)
        woT = sb("woT", [P, 2, D])
        wmean = sb("wmean", [P, 2, 2 * NH])
        rb = sb("rb", [P, NE])
        bo = sb("bo", [P, D])
        gb = sb("gb", [P, 4])
        gbr = sb("gbr", [1, 4, HS])
        bound = sb("bound", [1, 16])
        flag = sb("flag", [1, 1], I32)
        st = sb("st", [P, NT, 6])
        mv = sb("mv", [P, NT, 2])
        rstd = sb("rstd", [P, NT])
        mix = sb("mix", [P, 2 * D + 2 * GT * NE * NE])
        xn = mix[:, 0:2 * D].rearrange("p (s d) -> p s d", s=2)
        gt, eq = (mix[:, 2 * D + i * GT * NE * NE:2 * D + (i + 1) * GT * NE * NE].rearrange(
            "p (n e f) -> p n e f", n=GT, e=NE) for i in range(2))
        xt = sb("xt", [P, 2, 2, P])
        lg = sb("lg", [P, GT, NE])
        ex = sb("ex", [P, GT, NE])
        r3 = sb("r3", [P, 4, GT])
        rank = sb("rank", [P, GT, NE])
        wt = sb("wt", [P, NT, NE + 1])
        hw = sb("hw", [P, 2, NR + 1])
        hT = sb("hT", [NR + 1, 2, P])
        sq = ring[:, 0:2 * CH].rearrange("p (s c) -> p s c", s=2)
        qn = ring[:, 2 * CH:4 * CH].rearrange("p (s c) -> p s c", s=2)
        qT = ring[:, 4 * CH:6 * CH].rearrange("p (s c) -> p s c", s=2)
        qr = ring[:, 6 * CH:8 * CH].rearrange("p (s c) -> p s c", s=2)
        vr = ring[:, 8 * CH:9 * CH].rearrange("p (s c) -> p s c", s=2)
        ss = sb("ss", [P, 2, 2 * NH])
        opart = sb("opart", [P, 2, TC * VW])
        den = sb("den", [P, NT, NH])
        at = vhi_f[:, 0:2 * D * 2].bitcast(F32).rearrange("p (s d) -> p s d", s=2)
        atT = vhi_f[:, 2 * D * 2:4 * D * 2].bitcast(F32).rearrange("p (s a t) -> p s a t", s=2, a=2)
        mx2 = sb("mx2", [P, NT, 2])
        mx = sb("mx", [P, NT])
        mres = sb("mres", [P, 2, NT])
        mparts = sb("mparts", [P, PARTS, NT], BF16)
        mT = sb("mT", [PARTS * NT, P], BF16)

        ps = ctx.enter_context(nc.psum_tensor("ps", [P, 8 * CH], F32))

        def bank(b, n=1):
            return ps[:, b * CH:(b + n) * CH]

        bank_free = [None] * 8


        def mm(o, lhsT, rhs, start, stop, after=(), says=None):
            return pr.do("pe", lambda e: e.matmul(o, lhsT, rhs, start=start, stop=stop, skip_group_check=True), after, says)

        def tr(o, in_, idn, after=(), says=None):
            return pr.do("pe", lambda e: e.transpose(o, in_, idn), after, says)

        def act(o, in_, f, after=(), says=None, bias=0.0, scale=1.0):
            if f == ACTF.Copy:
                return pr.do("act", lambda e: e.activation(o, in_, f), after, says)
            return pr.do("act", lambda e: e.activation(o, in_, f, bias=bias, scale=scale), after, says)

        def tt(eng, o, a, b, op, after=(), says=None):
            return pr.do(eng, lambda e: e.tensor_tensor(o, a, b, op), after, says)

        def tsc(eng, o, a, s1, s2, op0, op1, after=(), says=None):
            if s2 is None:
                return pr.do(eng, lambda e: e.tensor_scalar(o, a, s1, None, op0), after, says)
            return pr.do(eng, lambda e: e.tensor_scalar(o, a, s1, s2, op0, op1), after, says)

        def stt(o, a, s, b, op0, op1, after=(), says=None):
            return pr.do("dve", lambda e: e.scalar_tensor_tensor(out=o, in0=a, scalar=s, in1=b, op0=op0, op1=op1), after, says)

        def red(o, a, op, after=(), says=None, absolute=False):
            if absolute:
                return pr.do("dve", lambda e: e.tensor_reduce(o, a, AX.X, op, apply_absolute_value=True), after, says)
            return pr.do("dve", lambda e: e.tensor_reduce(o, a, AX.X, op), after, says)

        def recip(o, a, after=(), says=None):
            return pr.do("dve", lambda e: e.reciprocal(o, a), after, says)

        def copy(eng, o, a, after=(), says=None):
            return pr.do(eng, lambda e: e.tensor_copy(o, a), after, says)

        def memset(eng, o, v, after=(), says=None):
            return pr.do(eng, lambda e: e.memset(o, v), after, says)

        def select(o, pattern, cm, base, op, fill, after=(), says=None):
            return pr.do("pool", lambda e: e.affine_select(out=o, in_=o, compare_op=op, fill=fill, base=base,
                                                           pattern=pattern, channel_multiplier=cm), after, says)

        z = memset("pool", ident[:, :], 0.0, says="const")
        ident_ok = select(ident[:, :], [[-1, P]], 1, 0, ALU.not_equal, 1.0, [z], "const")
        z = memset("pool", identb[:, :], 0.0, says="const")
        select(identb[:, :], [[-1, P]], 1, 0, ALU.not_equal, 1.0, [z], "const")
        z = memset("pool", maskT[:, :], 0.0, says="const")
        select(maskT[:, :], [[1, P]], -1, 0, ALU.is_ge, NEG, [z], "const")
        z = memset("pool", maskN[:, :], 0.0, says="const")
        select(maskN[:, :], [[-1, P]], 1, 0, ALU.is_ge, NEG, [z], "const")
        z = memset("pool", tri[:, :, :], 0.0, says="const")
        select(tri[:, :, :], [[-1, NE], [1, NE]], 0, 0, ALU.is_ge, 1.0, [z], "const")
        memset("pool", eps[:, :], EPS, says="const")
        memset("pool", wt[:, :, 0:1], 1.0, says="const")
        memset("pool", hw[:, :, NR:NR + 1], 1.0, says="const")
        const_ok = memset("pool", mT[:, :], 0.0, says="const")

        RAW_TILES = -(-7 * 2 * D * 2 // (NH * VW))

        def constant_columns(n0, n1, after=()):
            memset("pool", vhi[:, n0:n1, :, VO:VO + 1], 1.0, after, "v_ones")
            for r_ in range(1, PARTS):
                memset("pool", vhi[:, n0:n1, :, r_ * VL + HS:(r_ + 1) * VL], 0.0, [], "v_ones")

        constant_columns(RAW_TILES, NT)

        x_v = ap["x"][0].rearrange("(n p) d -> p n d", p=P)
        LT = 4
        x_in = []

        def load_x(i):
            x_in.append(pr.dma("sp", x[:, i * LT:(i + 1) * LT, :], x_v[:, i * LT:(i + 1) * LT, :], f"x_in{i}"))

        half = lambda w: w.rearrange("(b p) e -> p b e", p=P)
        A_RAW, B_RAW = 1, 2
        W_RAW = {"Wq": 3, "Wk": 4, "Wv": 5, "Wo": 6}
        raw_a = wraw[:, A_RAW, 0, :]
        raw_b = wraw[:, B_RAW, :, 0:NR]
        load_x(0)
        pr.dma("sp", raw_a[0:R, :], ap["shared_A"], "w_a")
        pr.dma("sp", raw_a[R:NR, :], ap["routed_A"].rearrange("e r d -> (e r) d"), "w_a")
        w_a = pr.dma("sp", raw_a[NR:NA, :], ap["router_W"], "w_a")
        load_x(1)
        w_base = pr.dma("sp", wraw[:, 0, :, :], half(ap["base_W"]), "w_base")
        for i in range(2, NT // LT):
            load_x(i)
        pr.dma("act", raw_b[:, :, 0:R], ap["shared_B"].rearrange("(b p) r -> p b r", p=P), "w_b")
        for e_ in range(NE):
            w_b = pr.dma("act", raw_b[:, :, R + e_ * R:R + (e_ + 1) * R],
                         ap["routed_B"][e_].rearrange("(b p) r -> p b r", p=P), "w_b")
        pr.dma("sp", rb[:, :], ap["router_b"].partition_broadcast(P), "w_vec")
        w_vec = pr.dma("sp", bo[:, :], ap["bo"].partition_broadcast(P), "w_vec")
        w_bias = pr.dma("sp", bT[NR:NR + 1, :], ap["base_b"].rearrange("(a n) -> a n", a=1), "w_bias")

        w_in = {name: pr.dma("sp", wraw[:, slot, :, :], half(ap[name]), f"w_in_{name}") for name, slot in W_RAW.items()}

        bank_turn = [0]

        def transpose_in(dst, src, rows, after, n_cols=P, by_act=False):
            b = bank_turn[0] % 4
            bank_turn[0] += 1
            t = tr(bank(b)[0:n_cols, 0:rows], src, ident[0:rows, 0:rows], list(after) + [bank_free[b]], "w_tr")
            bank_free[b] = (act(dst, bank(b)[0:n_cols, 0:rows], ACTF.Copy, [t], "w_cp_act") if by_act else
                            copy("dve", dst, bank(b)[0:n_cols, 0:rows], [t], "w_cp"))
            return bank_free[b]

        for ib in range(2):
            a_ready = transpose_in(aT[:, ib, :], raw_a[0:NA, ib * P:(ib + 1) * P], NA, [w_a, ident_ok])
        outer_ready = [None]

        def feed_forward_weights():
            for ob in range(2):
                for ib in range(2):
                    transpose_in(baseT[:, ib, ob * P:(ob + 1) * P], wraw[:, 0, ob, ib * P:(ib + 1) * P], P, [w_base, ident_ok])
                    for _ in range(SIDE // 2):
                        yield
            for _ in range(2 * SIDE):
                yield
            for ob in range(2):
                outer_ready[0] = transpose_in(bT[0:NR, ob * P:(ob + 1) * P], raw_b[:, ob, :], P, [w_b], NR)
                yield
            for _ in range(6 * SIDE):
                yield
            for _ in attention_weights():
                yield
            constant_columns(0, RAW_TILES, [("w_tr", pr.counts["w_tr"])])

        def attention_weights():
            for name, dst, off in (("Wq", qkT, 0), ("Wk", qkT, D), ("Wv", vT, 0), ("Wo", woT, 0)):
                for ob in range(2):
                    for ib in range(2):
                        m = transpose_in(dst[:, ib, off + ob * P:off + (ob + 1) * P],
                                         wraw[:, W_RAW[name], ob, ib * P:(ib + 1) * P], P, [w_in[name]], by_act=True)
                        yield
            for _ in range(8 * SIDE):
                yield
            a = red(wmean[:, :, :].rearrange("p a (h c) -> p (a h) c", c=1), qkT[:, :, :].rearrange("p a (h c) -> p (a h) c", c=HS), ALU.add, [m], "w_mean")
            yield
            a = pr.do("dve", lambda e: e.tensor_scalar_mul(wmean[:, :, :], wmean[:, :, :], 1.0 / HS), [a], "w_mean")
            for ib in range(2):
                yield
                tt("dve", qkT[:, ib, :].rearrange("p (h c) -> p h c", c=HS), qkT[:, ib, :].rearrange("p (h c) -> p h c", c=HS),
                   wmean[:, ib, :].unsqueeze(2).broadcast_to([P, 2 * NH, HS]), ALU.subtract, [a], "w_mean")

        def pipeline(stages, side=()):
            side = list(side)
            for t in range(NT + max(lag for lag, _ in stages)):
                for lag, stage in sorted(stages, key=lambda q: -q[0]):
                    if 0 <= t - lag < NT:
                        started = stage(t - lag)
                        if started is not None:
                            side.append(started)
                for _ in range(SIDE):
                    for q in list(side):
                        try:
                            next(q)
                        except StopIteration:
                            side.remove(q)
                yield

        def queue_steps(steps, count=None):
            for _ in (steps if count is None else zip(range(count), steps)):
                pass

        SIDE = 4
        sqrt_ok, rstd_ok = {}, {}

        def moments(n, ready):
            s = pr.do("dve", lambda e: e.bn_stats(st[:, n, :], x[:, n, :]), [ready[n]], "ln_st")
            if n % GT == GT - 1:
                for m in range(n - GT + 1, n + 1):
                    s2 = pr.do("dve", lambda e, m=m: e.bn_aggr(mv[:, m, :], st[:, m, :]), [s], "ln_st")
                sqrt_ok[n // GT] = act(rstd[:, n - GT + 1:n + 1], mv[:, n - GT + 1:n + 1, 1], ACTF.Sqrt, [s2, const_ok], "ln_sqrt", bias=eps[:, :])

        xn_free = [None, None]
        turn_banks = [0, 1]
        xn_ok, xnT_ok, xt_free = {}, {}, [None, None]

        def scale_tile(n):
            s, g = n % 2, n // GT
            if n % GT == 0:
                rstd_ok[g] = recip(rstd[:, n:n + GT], rstd[:, n:n + GT], [sqrt_ok[g]], "ln_r")
            xn_ok[n] = tsc("dve", xn[:, s, :], x[:, n, :], mv[:, n, 0:1], rstd[:, n:n + 1], ALU.subtract, ALU.mult,
                           [rstd_ok[n // GT], xn_free[s]], "xn")

        def turn_tile(n):
            s = n % 2
            b = turn_banks[s]
            for ib in range(2):
                t = tr(bank(b)[:, ib * P:(ib + 1) * P], xn[:, s, ib * P:(ib + 1) * P], ident[:, :], [xn_ok[n], bank_free[b]], "xn_tr")
            xn_free[s] = t
            xnT_ok[n] = bank_free[b] = act(xnT[:, :, n * P:(n + 1) * P], bank(b)[:, 0:2 * P].rearrange("p (a t) -> p a t", a=2),
                                           ACTF.Copy, [t], "xnT")

        out_v = out[0].rearrange("(n p) d -> p n d", p=P)

        def feed_forward(ready, final, banks, before=(), beside=(), behind=None):
            done = {}
            bank_a, bank_hw, bank_o = banks
            h_ok, wts, hw_ok, hT_ok = {}, {}, {}, {}
            hw_free, hT_free = [None, None], [None, None]

            def inner_a(n):
                for ib in range(2):
                    m = mm(bank(bank_a)[:, 0:NA], xnT[:, ib, n * P:(n + 1) * P], aT[:, ib, :], ib == 0, ib == 1,
                           [xnT_ok[n], a_ready, bank_free[bank_a]], "ff_a")
                h_ok[n] = bank_free[bank_a] = act(h_all[:, n, 0:NA], bank(bank_a)[:, 0:NA], ACTF.Copy, [m], "ff_h")
                return route(n // GT) if n % GT == GT - 1 else None

            ROUTE = 4
            def route(g):
                n0 = g * GT
                tiles = slice(n0, n0 + GT)
                a = tt("dve", lg[:, :, :], h_all[:, tiles, NR:NA], rb[:, :].unsqueeze(1).broadcast_to([P, GT, NE]), ALU.add, [h_ok[n0 + GT - 1], w_vec], "rt")
                yield
                a = red(r3[:, 0, :].unsqueeze(2), lg[:, :, :], ALU.max, [a], "rt")
                yield
                a = tt("dve", lg[:, :, :], lg[:, :, :], r3[:, 0, :].unsqueeze(2).broadcast_to([P, GT, NE]), ALU.subtract, [a], "rt")
                a = act(ex[:, :, :], lg[:, :, :], ACTF.Exp, [a], "rt_exp")
                for _ in range(SIDE):
                    yield
                red(r3[:, 1, :].unsqueeze(2), ex[:, :, :], ALU.add, [a], "rt")
                other = ex[:, :, :].unsqueeze(2).broadcast_to([P, GT, NE, NE])
                own = ex[:, :, :].unsqueeze(3).broadcast_to([P, GT, NE, NE])
                tt("dve", gt[:, :, :, :], other, own, ALU.is_gt, [a], "rt")
                a = tt("dve", eq[:, :, :, :], other, own, ALU.is_equal, [a], "rt")
                yield
                a = tt("dve", eq[:, :, :, :], eq[:, :, :, :], tri[:, :, :].unsqueeze(1).broadcast_to([P, GT, NE, NE]), ALU.mult, [a, const_ok], "rt")
                yield
                a = tt("dve", gt[:, :, :, :], gt[:, :, :, :], eq[:, :, :, :], ALU.add, [a], "rt")
                yield
                a = red(rank[:, :, :].unsqueeze(3), gt[:, :, :, :], ALU.add, [a], "rt")
                yield
                a = stt(rank[:, :, :], rank[:, :, :], 2.0, ex[:, :, :], ALU.is_lt, ALU.mult, [a], "rt")
                a = red(r3[:, 2, :].unsqueeze(2), rank[:, :, :], ALU.add, [a], "rt")
                yield
                a = stt(r3[:, 3, :], r3[:, 1, :], 1e-6, r3[:, 2, :], ALU.mult, ALU.add, [a], "rt")
                a = recip(r3[:, 3, :], r3[:, 3, :], [a], "rt")
                yield
                wts[g] = tt("dve", wt[:, tiles, 1:NE + 1], rank[:, :, :], r3[:, 3, :].unsqueeze(2).broadcast_to([P, GT, NE]), ALU.mult, [a], "rt")

            def weigh(n):
                s = n % 2
                hw_ok[n] = tt("pool", hw[:, s, 0:NR].rearrange("p (e r) -> p e r", r=R), h_all[:, n, 0:NR].rearrange("p (e r) -> p e r", r=R),
                              wt[:, n, :].unsqueeze(2).broadcast_to([P, NE + 1, R]), ALU.mult, [wts[n // GT], hw_free[s]], "ff_w")

            def turn_inner(n):
                s = n % 2
                hw_free[s] = t = tr(bank(bank_hw)[0:NR + 1, 0:P], hw[:, s, :], ident[:, :], [hw_ok[n], bank_free[bank_hw]], "ff_tr")
                hT_ok[n] = bank_free[bank_hw] = act(hT[:, s, :], bank(bank_hw)[0:NR + 1, 0:P], ACTF.Copy, [t, hT_free[s]], "ff_hT")

            def outer(n):
                s = n % 2
                b = bank_o[s]
                mm(bank(b)[:, 0:D], xnT[:, 0, n * P:(n + 1) * P], baseT[:, 0, :], True, False, [bank_free[b], outer_ready[0]])
                mm(bank(b)[:, 0:D], xnT[:, 1, n * P:(n + 1) * P], baseT[:, 1, :], False, False)
                m = hT_free[s] = mm(bank(b)[:, 0:D], hT[:, s, :], bT[:, :], False, True, [hT_ok[n], w_bias], "ff_o")
                done[n] = bank_free[b] = stt(x[:, n, :], bank(b)[:, 0:D], 0.5, x[:, n, :], ALU.mult, ALU.add, [m], "ff_x")
                if final and n % 2 == 1:
                    pr.dma("sp", out_v[:, n - 1:n + 1, :], x[:, n - 1:n + 1, :], "out", [done[n]])

            start = 1 + max([lag for lag, _ in before], default=-1)
            a = start + GT + 1
            b = a + 3 + GT + ROUTE
            steps = pipeline(list(before) + [(start, lambda n: moments(n, ready)), (a, scale_tile), (a + 1, turn_tile), (a + 3, inner_a),
                                     (b, weigh), (b + 1, turn_inner), (b + 3, outer)] +
                     ([] if behind is None else [(start + GT * -(-(b + 4 - start) // GT), behind(done))]), beside)
            return done, steps

        for i, name in enumerate(["qln_g", "qln_b", "kln_g", "kln_b"]):
            for h in range(P // HS):
                pr.dma("sp", gb[h * HS:(h + 1) * HS, i:i + 1], ap[name].rearrange("(a n) -> a n", n=1), "gb_in")
            gb_in = pr.dma("sp", gbr[:, i, :], ap[name].rearrange("(a n) -> a n", a=1), "gb_in")
        for h in range(NH):
            shift_zero = pr.dma("sp", shift_d[h].rearrange("r (n t) -> (r n) t", t=P), mT[:, :], "shift_in", [const_ok])

        x1, ff_steps = feed_forward({n: x_in[n // LT] for n in range(NT)}, False, (2, 6, (4, 5)), beside=[feed_forward_weights()],
                                    behind=lambda x1: lambda n: moments(n, x1))
        DRAIN = 8
        queue_steps(ff_steps, NT + 20 - DRAIN)
        sc = pr.do("dve", lambda e: e.tensor_scalar_mul(gb[:, :], gb[:, :], SCALE), [gb_in], "bnd")
        flag_ok = []

        def bound_scores():
            m = red(bound[:, 0:4].unsqueeze(2), gbr[:, :, :], ALU.max, [gb_in], "bnd", absolute=True)
            yield
            m = tt("dve", gbr[:, :, :], gbr[:, :, :], gbr[:, :, :], ALU.mult, [m], "bnd")
            yield
            m = red(bound[:, 4:8].unsqueeze(2), gbr[:, :, :], ALU.add, [m], "bnd")
            yield
            m = act(bound[:, 8:12], bound[:, 4:8], ACTF.Sqrt, [m], "bnd_sqrt")
            for _ in range(SIDE):
                yield
            bv = bound[:, :].rearrange("a (k b c) -> a k b c", k=4, c=2)
            m = stt(bound[:, 12:14], bv[:, 0, :, 0], float(HS) ** 0.5, bv[:, 2, :, 1], ALU.mult, ALU.add, [m], "bnd")
            yield
            m = tt("dve", bound[:, 14:15], bound[:, 12:13], bound[:, 13:14], ALU.mult, [m], "bnd")
            yield
            limit = -1.0 if always_general else SAFE
            m = tsc("dve", bound[:, 15:16], bound[:, 14:15], SCALE * SCALE, limit, ALU.mult, ALU.is_le, [m], "bnd")
            yield
            flag_ok.append(copy("dve", flag[:, :], bound[:, 15:16], [m], "bnd"))

        v_ones = ("v_ones", pr.counts["v_ones"])
        w_turned = ("w_cp_act", pr.counts["w_cp_act"])
        w_centred = ("w_mean", pr.counts["w_mean"])

        def load_operands(h, sem, after, shift=True, t0=0, t1=T):
            slot, blk, row = h % 2, h // 8, (h % 8) * HS
            for i, (a_, b_) in enumerate(zip(Q_PARTS, K_PARTS)):
                pr.dma("sp", ops[i * HS:(i + 1) * HS, slot, 0, t0:t1], parts_d[a_, blk, row:row + HS, t0:t1], sem, after)
                mk = pr.dma("sp", ops[i * HS:(i + 1) * HS, slot, 1, t0:t1], parts_d[b_, 2 + blk, row:row + HS, t0:t1], sem, after)
            if shift:
                mk = pr.dma("sp", ops[KR:KS, slot, 0, t0:t1], shift_d[h][:, t0:t1], sem, after)
            return mk

        ones_rows = []

        def ones_side():
            for _ in range(12 * SIDE):
                yield
            ff_pe = ("ff_o", pr.counts["ff_o"])
            for slot in range(2):
                for c in range(0, T, T // 4):
                    ones_rows.append(act(ops[KR:KS, slot, 1, c:c + T // 4], wt[KR:KS, 0, 0:1].broadcast_to([PARTS, T // 4]), ACTF.Copy,
                                         [ff_pe, const_ok], "ones"))
                    for _ in range(SIDE):
                        yield

        op_ready = {}
        parts_ok = {}
        BLOCKS = {0: 1, 1: 4}

        def fetch_first(c):
            for h, k in BLOCKS.items():
                if c % k == k - 1:
                    mk = load_operands(h, f"op_first{h}_{c // k}", [parts_ok[i] for i in range(c - k + 1, c + 1)] + [("ff_o", pr.counts["ff_o"]), shift_zero],
                                       t0=(c - k + 1) * CH, t1=(c + 1) * CH)
                    for i in range(c - k + 1, c + 1):
                        op_ready[(h, i)] = mk

        stage_free = [None, None]
        sq_f, qn_f, qT_f, qr_f, vr_f, ss_f = ([None, None] for _ in range(6))
        ss_ok, qn_ok, qT_ok, qr_ok, vr_ok, v_ok = {}, {}, {}, {}, {}, {}
        heads = lambda t_: t_.rearrange("p (h c) -> p h c", c=HS)

        def turn_tile_small(n):
            s = n % 2
            for ib in range(2):
                t = tr(bank(s)[:, ib * P:(ib + 1) * P], xn[:, s, ib * P:(ib + 1) * P], ident[:, :], [xn_ok[n], bank_free[s]], "xn_tr")
            xn_free[s] = t
            xnT_ok[n] = bank_free[s] = act(xt[:, s, :, :], bank(s)[:, 0:2 * P].rearrange("p (a t) -> p a t", a=2),
                                           ACTF.Copy, [t, xt_free[s]], "xnT")

        def project_qkv(n):
            s = n % 2
            b = 2 + s
            for ib in range(2):
                m = mm(bank(b), xt[:, s, ib, :], qkT[:, ib, :], ib == 0, ib == 1, [xnT_ok[n], w_centred, w_turned, bank_free[b]], "qk")
            for ib in range(2):
                mv_ = xt_free[s] = mm(bank(4 + s)[:, 0:D], xt[:, s, ib, :], vT[:, ib, :], ib == 0, ib == 1, [bank_free[4 + s]], "v")
            a = act(sq[:, s, :], bank(b), ACTF.Square, [m, sq_f[s]], "qk_sq")
            ss_ok[n] = sq_f[s] = red(ss[:, s, :].unsqueeze(2), heads(sq[:, s, :]), ALU.add, [a, ss_f[s]], "qk_ss")
            v0 = heads(bank(4 + s)[:, 0:D])
            a = act(vhi[:, n, :, 0:HS], v0, ACTF.Copy, [mv_, v_ones], "vcut_a")
            vr_ok[n] = bank_free[4 + s] = tt("dve", heads(vr[:, s, :]), v0, vhi[:, n, :, 0:HS], ALU.subtract, [a, vr_f[s]], "vcut_d")

        def scale_heads(n):
            s = n % 2
            b = 2 + s
            a = act(ss[:, s, :], ss[:, s, :], ACTF.Sqrt, [ss_ok[n]], "qk_rt", bias=eps[:, :], scale=1.0 / HS)
            a = recip(ss[:, s, :], ss[:, s, :], [a], "qk_ss")
            qn_ok[n] = bank_free[b] = ss_f[s] = tt("dve", heads(qn[:, s, :]), heads(bank(b)), ss[:, s, :].unsqueeze(2).broadcast_to([P, 2 * NH, HS]),
                                                   ALU.mult, [a, qn_f[s]], "qk_n")

        def turn_heads(n):
            s = n % 2
            b = 6 + s
            for k in range(4):
                t = tr(bank(b)[:, k * P:(k + 1) * P], qn[:, s, k * P:(k + 1) * P], ident[:, :], [qn_ok[n], bank_free[b]], "qk_tr")
            qn_f[s] = t
            tsc("dve", qT[:, s, 0:2 * P], bank(b)[:, 0:2 * P], gb[:, 0:1], gb[:, 1:2], ALU.mult, ALU.add, [t, qT_f[s], sc], "qk_T")
            qT_ok[n] = bank_free[b] = tsc("dve", qT[:, s, 2 * P:], bank(b)[:, 2 * P:], gb[:, 2:3], gb[:, 3:4], ALU.mult, ALU.add, [t], "qk_T")
            a = act(vhi[:, n, :, VL:VL + HS], heads(vr[:, s, :]), ACTF.Copy, [vr_ok[n]], "vcut_a")
            v_ok[n] = vr_f[s] = tt("pool", vhi[:, n, :, 2 * VL:2 * VL + HS], heads(vr[:, s, :]), vhi[:, n, :, VL:VL + HS], ALU.subtract, [a], "vcut_p")

        cutter = lambda n: ("dve", "cut_d") if n >= NT - LATE_CUTS else ("pool", "cut_p")
        LATE_CUTS = 2

        def round_to(n, o, a, after):
            if n == NT - 1:
                return copy("dve", o, a, after, "cut_v")
            return act(o, a, ACTF.Copy, after, "cut_a")

        def staged(n, i):
            return stage[:, (n // TC) % 2, i, :, (n % TC) * P:(n % TC + 1) * P]

        def cut_first(n):
            s = n % 2
            full = qT[:, s, :].rearrange("p (b t) -> p b t", b=4)
            left = qr[:, s, :].rearrange("p (b t) -> p b t", b=4)
            a = round_to(n, staged(n, 0), full, [qT_ok[n], stage_free[(n // TC) % 2]])
            eng, says = cutter(n)
            qr_ok[n] = qT_f[s] = tt(eng, left, full, staged(n, 0), ALU.subtract, [a, qr_f[s]], says)

        def cut_rest(n):
            s, sg = n % 2, (n // TC) % 2
            left = qr[:, s, :].rearrange("p (b t) -> p b t", b=4)
            a = round_to(n, staged(n, 1), left, [qr_ok[n]])
            eng, says = cutter(n)
            a = qr_f[s] = tt(eng, staged(n, 2), left, staged(n, 1), ALU.subtract, [a], says)
            if n % TC == TC - 1:
                c0 = (n // TC) * CH
                pr.wait("sp", ("cut_p", pr.counts["cut_p"]))
                for i in range(PARTS):
                    parts_ok[n // TC] = stage_free[sg] = pr.dma("sp", parts_d[i, :, :, c0:c0 + CH].rearrange("b p t -> p b t"), stage[:, sg, i, :, :],
                                            f"parts{sg}", [a])
                if n // TC >= 1:
                    fetch_first(n // TC - 1)

        qkv_steps = pipeline([(0, scale_tile), (1, turn_tile_small), (3, project_qkv), (4, scale_heads),
                              (5, turn_heads), (6, cut_first), (7, cut_rest)], [bound_scores(), ones_side()])
        for _ in range(DRAIN):
            queue_steps(ff_steps, 1)
            queue_steps(qkv_steps, 1)
        queue_steps(ff_steps)
        queue_steps(qkv_steps)
        fetch_first(NC - 1)

        bo_ok = {}

        def add_bo(n):
            bo_ok[n] = tt("pool", x[:, n, :], x[:, n, :], bo[:, :], ALU.add, [x1[n], rstd_ok[NT // GT - 1], w_vec, xn_free[0], xn_free[1]], "x_bo")

        prep_pe = [("qk", pr.counts["qk"]), ("v", pr.counts["v"])]
        parts_all = [stage_free[0], stage_free[1]]

        engines = ["pe", "dve", "sp"]
        for e_ in engines:
            pr.wait(e_, flag_ok[0])
            pr.only_if_zero(e_, flag[0:1, 0:1])
        slot_free = [None, None]
        first_ok = [op_ready[q] for q in sorted(op_ready)]
        reg_free = [[bank_free[i] for i in range(4)], [bank_free[i] for i in range(4, 8)]]
        turn = 0
        mT_free = shift_zero
        mp_free = None
        for h in range(NH):
            s = h % 2
            ready = load_operands(h, f"gen_in{s}", parts_all + prep_pe + first_ok + [slot_free[s]], shift=False)
            last = None
            for n in range(NT):
                width = (n + 1) * P
                for k, j0 in enumerate(range(0, width, 4 * CH)):
                    w = min(4 * CH, width - j0)
                    region = bank(4 * (turn % 2), 4)
                    for c0 in range(0, w, CH):
                        cw = min(CH, w - c0)
                        diag = j0 + c0 + cw == width
                        m = mm(region[:, c0:c0 + cw], ops[0:KR, s, 0, n * P:(n + 1) * P], ops[0:KR, s, 1, j0 + c0:j0 + c0 + cw],
                               True, not diag, [ready] + reg_free[turn % 2], None if diag else "gen_mm")
                        if diag:
                            m = mm(region[:, c0 + cw - P:c0 + cw], identb[:, :], maskN[:, :], False, True, [], "gen_mm")
                    last = red(mx2[:, n, k:k + 1], region[:, 0:w], ALU.max, [m, mp_free], "gen_max")
                    reg_free[turn % 2] = [last]
                    turn += 1
            slot_free[s] = m
            two = NT // 2
            copy("dve", mx[:, 0:two], mx2[:, 0:two, 0], [last], "gen_v")
            a = tt("dve", mx[:, two:], mx2[:, two:, 0], mx2[:, two:, 1], ALU.max, [last], "gen_v")
            a = tsc("dve", mres[:, 0, :], mx[:, :], -1.0, None, ALU.mult, None, [a], "gen_v")
            a = copy("dve", mparts[:, 0, :], mres[:, 0, :], [a], "gen_v")
            a = tt("dve", mres[:, 1, :], mres[:, 0, :], mparts[:, 0, :], ALU.subtract, [a], "gen_v")
            a = copy("dve", mparts[:, 1, :], mres[:, 1, :], [a], "gen_v")
            a = tt("dve", mparts[:, 2, :], mres[:, 1, :], mparts[:, 1, :], ALU.subtract, [a], "gen_v")
            mp_free = a
            b = 4 * (turn % 2)
            t = tr(bank(b)[0:PARTS * NT, 0:P // 2].bitcast(BF16), mparts[:, :, :].rearrange("p r n -> p (r n)"), identb[:, :],
                   [a] + reg_free[turn % 2], "gen_tr")
            a = copy("dve", mT[:, :], bank(b)[0:PARTS * NT, 0:P // 2].bitcast(BF16), [t, mT_free], "gen_v")
            reg_free[turn % 2] = [a]
            turn += 1
            mT_free = pr.dma("sp", shift_d[h].rearrange("r (n t) -> (r n) t", t=P), mT[:, :], "gen_out", [a])
        for h in range(2):
            pr.wait("pe", load_operands(h, f"gen_in{h}", [slot_free[h], mT_free]))
        pr.wait("pe", *reg_free[0], *reg_free[1])
        for e_ in engines:
            pr.end_if(e_)

        units, banks = [], []
        for h in range(NH):
            for c in range(NC):
                d = TC * c
                banks += [[(h, c, j, 0, CH, 0)] for j in range(d + 1)]
                banks.append([(h, c, d + 1, P, 3 * P, 0), (h, c, d + 3, 3 * P, P, 3 * P)])
                if c % 2 == 0:
                    banks.append([(h, c, d + 2, 2 * P, 2 * P, 0), (h, c + 1, d + TC + 2, 2 * P, 2 * P, 2 * P)])
        for i in range(0, len(banks), UB):
            assert all(sum(q[4] for q in bk) == CH for bk in banks[i:i + UB])
            units.append([(q[:5] + (k * CH + q[5],)) for k, bk in enumerate(banks[i:i + UB]) for q in bk])
        seq_first, seq_last = {}, {}
        for u, un in enumerate(units):
            for i, q in enumerate(un):
                seq_first.setdefault((q[0], q[1]), (u, i))
                seq_last[(q[0], q[1])] = (u, i)

        op_free = [None, None]
        scratch_done = [None, qT_f, qr_f + vr_f]

        def fetch(h):
            op_ready.update({(h, c): None for c in range(1, NC)})
            op_ready[(h, 0)] = load_operands(h, f"op_in{h % 2}", parts_all + [shift_zero] + list(op_free[h % 2]))

        unit_free = [[bank_free[i] for i in range(3)], [bank_free[i] for i in range(3, 6)]]
        acc_free = [bank_free[6], bank_free[7]]
        s_done, e_done, r_done, pv_done = {}, {}, {}, {}
        UPPER = 1

        def scores(u):
            for i, (h, c, j, c0, w, col) in enumerate(units[u]):
                o = bank(3 * (u % 2), UB)[:, col:col + w]
                diag = j >= TC * c
                last_in = i == len(units[u]) - 1
                q0 = c * CH + c0
                m = mm(o, ops[0:KS, h % 2, 1, j * P:(j + 1) * P], ops[0:KS, h % 2, 0, q0:q0 + w],
                       col % CH == 0, not diag, [op_ready[(h, c)], ones_rows[-1]] + unit_free[u % 2], None if diag or not last_in else "s")
                if diag:
                    m = mm(o[:, 0:P], identb[:, :], maskT[:, :], False, True, [], "s" if last_in else None)
            s_done[u] = m

        def exps(u):
            e_done[u] = act(probs[:, u % 3, :], bank(UB * (u % 2), UB), ACTF.Exp,
                            [s_done[u], pv_done.get(u - 3)] + (scratch_done[u] or [] if u < 3 else []), "exp")
            unit_free[u % 2] = [e_done[u]]

        def rests(u):
            r_done[u] = tt("dve", rest[:, u % 3, :], probs[:, u % 3, :], halves[:, u % 3, :, UPPER], ALU.subtract,
                           [e_done[u], pv_done.get(u - 3)], "rest")

        acc_of = {}
        pending = []

        part_free = [None, None]
        o_ok = {}

        def finish_chunk(h, c, acc, complete):
            acc_free[acc] = a = act(opart[:, acc, :], bank(6 + acc)[:, 0:TC * VW], ACTF.Copy, [complete, part_free[acc]], "o_ev")
            part = opart[:, acc, :].rearrange("p (k r c) -> p r k c", k=TC, r=PARTS)
            to = o_all[:, TC * c:TC * (c + 1), h, :]
            a = tt("pool", to, part[:, 0], part[:, 1], ALU.add, [a] + parts_all, "o_cp")
            part_free[acc] = tt("pool", to, to, part[:, 2], ALU.add, [a], "o_cp")
            if h == NH - 1:
                for n in range(TC * c, TC * (c + 1)):
                    o_ok[n] = part_free[acc]

        def values(u):
            for i, (h, c, j, c0, w, col) in enumerate(units[u]):
                first = seq_first[(h, c)] == (u, i)
                if first:
                    acc_of[(h, c)] = len(acc_of) % 2
                    while pending and pending[0][2] == acc_of[(h, c)]:
                        finish_chunk(*pending.pop(0))
                acc = acc_of[(h, c)]
                last = seq_last[(h, c)] == (u, i)
                for k in range(w // P):
                    tile = c0 // P + k
                    o = bank(6 + acc)[:, tile * VW:(tile + 1) * VW]
                    cols = slice(col + k * P, col + (k + 1) * P)
                    ends = k == w // P - 1
                    mm(o, halves[:, u % 3, cols, UPPER], vhi[:, j, h, :], first and k == 0, False,
                       [r_done[u], v_ok[j], acc_free[acc] if first else None])
                    m = mm(o, rest[:, u % 3, cols], vhi[:, j, h, :], False, last and ends, [],
                           "pv" if ends and (last or i == len(units[u]) - 1) else None)
                if last:
                    pending.append((h, c, acc, m))
                    if c == NC - 1:
                        op_free[h % 2] = [s_done[u]] if u + 1 not in s_done else [s_done[u + 1]]
                        if h + 2 < NH:
                            fetch(h + 2)
            pv_done[u] = m

        x2, at_ok, atT_ok = {}, {}, {}
        at_f, atT_f = [None, None], [None, None]
        den_ok = {}

        def over_sum(n):
            s = n % 2
            g = n // GT
            if g not in den_ok:
                den_ok[g] = recip(den[:, g * GT:(g + 1) * GT, :], o_all[:, g * GT:(g + 1) * GT, :, VO], [o_ok[n]], "o_n")
            at_ok[n] = tt("dve", heads(at[:, s, :]), o_all[:, n, :, 0:HS],
                          den[:, n, :].unsqueeze(2).broadcast_to([P, NH, HS]), ALU.mult, [o_ok[n], den_ok[g], at_f[s], at_place], "o_n")

        def turn_out(n):
            s = n % 2
            for ib in range(2):
                t = tr(bank(0)[:, ib * P:(ib + 1) * P], at[:, s, ib * P:(ib + 1) * P], ident[:, :], [at_ok[n], bank_free[0]], "o_tr")
            at_f[s] = t
            atT_ok[n] = bank_free[0] = act(atT[:, s, :, :], bank(0)[:, 0:2 * P].rearrange("p (a t) -> p a t", a=2), ACTF.Copy, [t, atT_f[s]], "o_T")

        def project_out(n):
            s = n % 2
            b = 2 if n % 2 == 1 and n < 12 else 1
            for ib in range(2):
                m = mm(bank(b)[:, 0:D], atT[:, s, ib, :], woT[:, ib, :], ib == 0, ib == 1, [atT_ok[n], bank_free[b]], "o_p")
            atT_f[s] = m
            x2[n] = bank_free[b] = tt("dve", x[:, n, :], bank(b)[:, 0:D], x[:, n, :], ALU.add, [m, bo_ok[n]], "o_x")

        NU = len(units)
        assert (NU - 1) % 2 == 1
        post_steps = None
        scores(0)
        for u in range(NU):
            exps(u)
            if u == NU - 1:
                for b in range(3):
                    bank_free[b] = e_done[u - 1]
                assert all(q[2] >= 3 for un in units[NU - 4:] for q in un)
                at_place = pv_done[NU - 5]
                turn_banks[:] = [6, 7]
                _, post_steps = feed_forward(x2, True, (3, 4, (5, 2)),
                                             before=[(0, over_sum), (2, turn_out), (4, project_out)])
                queue_steps(post_steps, 1)
            if pending and u >= 2:
                finish_chunk(*pending.pop(0))
            rests(u)
            if u % 4 == 2 and u // 4 < NT:
                add_bo(u // 4)
            if u + 1 < NU:
                scores(u + 1)
            if post_steps:
                queue_steps(post_steps, 1)
            if u >= 1:
                values(u - 1)
            if post_steps:
                queue_steps(post_steps, 1)
        values(NU - 1)
        while pending:
            finish_chunk(*pending.pop(0))
        for b in range(3, 8):
            bank_free[b] = e_done[NU - 1] if b < 6 else acc_free[b - 6]
        queue_steps(post_steps)
        pr.wait("sp", ("out", pr.counts["out"]))

        block = ctx.enter_context(nc.Block())

        @block.sync
        def _(e):
            pr.emit("sp", e)

        @block.gpsimd
        def _(e):
            pr.emit("pool", e)

        @block.scalar
        def _(e):
            pr.emit("act", e)

        @block.vector
        def _(e):
            pr.emit("dve", e)

        @block.tensor
        def _(e):
            pr.emit("pe", e)


INPUTS = {
    "L0_attn_x": "x", "L0_attn_Wk": "Wk", "L0_attn_Wq": "Wq", "L0_attn_Wv": "Wv", "L0_attn_Wo": "Wo", "L0_attn_bo": "bo",
    "L0_attn_kln_g": "kln_g", "L0_attn_kln_b": "kln_b", "L0_attn_qln_g": "qln_g", "L0_attn_qln_b": "qln_b",
    "L0_ffn_base_W": "base_W", "L0_ffn_base_b": "base_b", "L0_ffn_shared_A": "shared_A", "L0_ffn_shared_B": "shared_B",
    "L0_ffn_routed_A": "routed_A", "L0_ffn_routed_B": "routed_B", "L0_ffn_router_W": "router_W", "L0_ffn_router_b": "router_b",
}


def kernel(**inputs):
    import numpy as np
    import concourse.bacc as bacc
    from concourse.bass_utils import run_bass_kernel_spmd

    nc = bacc.Bacc("TRN2", target_bir_lowering=False, num_devices=1)
    arrays, aps = {}, {}
    for name, short in INPUTS.items():
        a = np.ascontiguousarray(inputs[name])
        arrays[f"in_{short}"] = a
        aps[short] = nc.dram_tensor(f"in_{short}", a.shape, mybir.dt.from_np(a.dtype), kind="ExternalInput").ap()
    shape = tuple(inputs["L0_attn_x"].shape)
    out = nc.dram_tensor("out_x", shape, F32, kind="ExternalOutput").ap()
    build(nc, aps, out)
    r = run_bass_kernel_spmd(nc, [arrays], core_ids=[0])
    return r.results[0]["out_x"]
```
